# Optimizing a Trainium2 kernel written in Bass

```python
import numpy as np
import jax
import jax.numpy as jnp

def _softmax(x, axis=-1):
    return jax.nn.softmax(x, axis=axis)

def _gelu(x):
    return jax.nn.gelu(x, approximate=True)

def _silu(x):
    return jax.nn.silu(x)

def _sigmoid(x):
    return jax.nn.sigmoid(x)

def _layernorm(x, axis=-1, eps=1e-05):
    m = jnp.mean(x, axis=axis, keepdims=True)
    v = jnp.var(x, axis=axis, keepdims=True)
    return (x - m) / jnp.sqrt(v + eps)

def _scatter_add(tgt, idx, src, axis=0):
    return tgt.at[idx].add(src)

def _segment_sum(src, seg, n):
    return jax.ops.segment_sum(src, seg, n)
kernel_name = 'mk_macaron_d4_jaxref_r8_e0c879'

def setup_inputs(seed: int=0):
    np.random.seed(seed)
    _w = jnp.asarray

    def _L0_attn_setup():
        import jax, jax.numpy as jnp
        import numpy as np
        DIM, SSM, RNN = (128, 64, 128)
        key = jax.random.key(seed)
        ks = jax.random.split(key, 16)
        s = 0.02
        B, N = (8, 256)
        return {'x': jax.random.normal(ks[0], (B, N, DIM), jnp.float32), 'A': jax.random.normal(ks[1], (SSM, SSM), jnp.float32) * s, 'Bw': jax.random.normal(ks[2], (SSM, DIM), jnp.float32) * s, 'Bb': jnp.zeros((SSM,), jnp.float32), 'Cw': jax.random.normal(ks[3], (DIM, SSM), jnp.float32) * s, 'Cb': jnp.zeros((DIM,), jnp.float32), 'Dw': jax.random.normal(ks[4], (DIM, DIM), jnp.float32) * s, 'Db': jnp.zeros((DIM,), jnp.float32), 'W_ih': jax.random.normal(ks[5], (3 * RNN, DIM), jnp.float32) * s, 'b_ih': jnp.zeros((3 * RNN,), jnp.float32), 'W_hh': jax.random.normal(ks[6], (3 * RNN, RNN), jnp.float32) * s, 'b_hh': jnp.zeros((3 * RNN,), jnp.float32), 'proj_w': jax.random.normal(ks[7], (DIM, RNN), jnp.float32) * s, 'proj_b': jnp.zeros((DIM,), jnp.float32), 'gate_w': jax.random.normal(ks[8], (2, DIM), jnp.float32) * s, 'gate_b': jnp.zeros((2,), jnp.float32)}
    _L0_attn_in = _L0_attn_setup()

    def _L0_ffn_setup():
        import jax, jax.numpy as jnp
        import numpy as np
        B, S, D_MODEL, D_FF = (4, 256, 128, 512)

        def _quantum_transform(hidden, theta, w_real, w_imag):
            imag = w_imag * jnp.sin(theta + hidden * 0.1)
            quantum_phase = jnp.cos(theta) * w_real + jnp.sin(theta) * w_imag
            return hidden + quantum_phase * imag * 0.1
        key = jax.random.key(seed)
        ks = jax.random.split(key, 8)
        return {'x': jax.random.normal(ks[0], (B, S, D_MODEL), dtype=jnp.float32), 'W1': jax.random.normal(ks[1], (D_MODEL, D_FF), dtype=jnp.float32) * (1.0 / np.sqrt(D_MODEL)), 'b1': jnp.zeros((D_FF,), dtype=jnp.float32), 'quantum_phases': jax.random.normal(ks[2], (D_FF,), dtype=jnp.float32) * (2.0 * np.pi), 'quantum_weights_real': jax.random.normal(ks[3], (D_FF,), dtype=jnp.float32) * 0.1, 'quantum_weights_imag': jax.random.normal(ks[4], (D_FF,), dtype=jnp.float32) * 0.1, 'W2': jax.random.normal(ks[5], (D_FF, D_MODEL), dtype=jnp.float32) * (1.0 / np.sqrt(D_FF)), 'b2': jnp.zeros((D_MODEL,), dtype=jnp.float32)}
    _L0_ffn_in = _L0_ffn_setup()

    def _L1_attn_setup():
        import jax, jax.numpy as jnp
        import numpy as np
        HID = 128
        NH = 4
        DK = 32
        DV = 64
        C = 64
        EPS = 1e-05
        GLN = 16.0

        def _xavier(key, shape, gain=2 ** (-2.5)):
            fan_in, fan_out = shape
            lim = gain * np.sqrt(6.0 / (fan_in + fan_out))
            return jax.random.uniform(key, shape, jnp.float32, -lim, lim)

        def _chunk_simple_gla(q, k, v, g):
            B, H, N, dk = q.shape
            dv = v.shape[-1]
            nc = N // C
            scale = dk ** (-0.5)
            q = q.reshape(B, H, nc, C, dk) * scale
            k = k.reshape(B, H, nc, C, dk)
            v = v.reshape(B, H, nc, C, dv)
            g = g.reshape(B, H, nc, C)
            gc = jnp.cumsum(g, axis=-1)
            gt = gc[..., -1]
            dec = gc[..., :, None] - gc[..., None, :]
            mask = jnp.tril(jnp.ones((C, C), bool))
            A = jnp.einsum('bhntd,bhnsd->bhnts', q, k)
            A = A * jnp.where(mask, jnp.exp(jnp.where(mask, dec, 0.0)), 0.0)
            o_intra = jnp.einsum('bhnts,bhnsd->bhntd', A, v)
            qs = jnp.moveaxis(q, 2, 0)
            ks_ = jnp.moveaxis(k, 2, 0)
            vs = jnp.moveaxis(v, 2, 0)
            gcs = jnp.moveaxis(gc, 2, 0)
            gts = jnp.moveaxis(gt, 2, 0)
            S0 = jnp.zeros((B, H, dk, dv), q.dtype)

            def step(S, inp):
                qc, kc, vc, gcc, gtc = inp
                o_int = jnp.einsum('bhtd,bhde->bhte', qc * jnp.exp(gcc)[..., None], S)
                kd = kc * jnp.exp(gtc[..., None] - gcc)[..., None]
                S = jnp.exp(gtc)[..., None, None] * S + jnp.einsum('bhtd,bhte->bhde', kd, vc)
                return (S, o_int)
            _, o_inter = jax.lax.scan(step, S0, (qs, ks_, vs, gcs, gts))
            o = o_intra + jnp.moveaxis(o_inter, 0, 2)
            return o.reshape(B, H, N, dv)
        key = jax.random.key(seed)
        ks = jax.random.split(key, 8)
        x = jax.random.normal(ks[0], (4, 256, HID), jnp.float32)
        Wq = _xavier(ks[1], (HID, NH * DK))
        Wk = _xavier(ks[2], (HID, NH * DK))
        Wv = _xavier(ks[3], (HID, NH * DV))
        Wg = _xavier(ks[4], (HID, NH * DV))
        Wgk = _xavier(ks[5], (HID, NH))
        bgk = jnp.zeros((NH,), jnp.float32)
        Wo = _xavier(ks[6], (NH * DV, HID))
        gnorm_w = jnp.ones((DV,), jnp.float32)
        return {'x': x, 'Wq': Wq, 'Wk': Wk, 'Wv': Wv, 'Wg': Wg, 'Wgk': Wgk, 'bgk': bgk, 'Wo': Wo, 'gnorm_w': gnorm_w}
    _L1_attn_in = _L1_attn_setup()

    def _L1_ffn_setup():
        import jax, jax.numpy as jnp
        import numpy as np
        NUM_EXPERTS = 8
        TOP_K = 2
        key = jax.random.key(seed)
        ks = jax.random.split(key, 4)
        B, S, D, F = (4, 256, 128, 512)
        E = NUM_EXPERTS
        x = jax.random.normal(ks[0], (B, S, D), dtype=jnp.float32)
        gate_w = jax.random.normal(ks[1], (D, E), dtype=jnp.float32) * 0.02
        gate_b = jnp.zeros((E,), dtype=jnp.float32)
        W1 = jax.random.normal(ks[2], (E, D, F), dtype=jnp.float32) * 0.02
        b1 = jnp.zeros((E, F), dtype=jnp.float32)
        W2 = jax.random.normal(ks[3], (E, F, D), dtype=jnp.float32) * 0.02
        b2 = jnp.zeros((E, D), dtype=jnp.float32)
        return {'x': x, 'gate_w': gate_w, 'gate_b': gate_b, 'W1': W1, 'b1': b1, 'W2': W2, 'b2': b2}
    _L1_ffn_in = _L1_ffn_setup()

    def _L2_attn_setup():
        import jax, jax.numpy as jnp
        import numpy as np
        WINDOW = 64
        SHIFT = 32
        HEADS = 8
        key = jax.random.key(seed)
        k1, k2, k3 = jax.random.split(key, 3)
        B, L, D = (8, 512, 128)
        scale = 0.02
        return {'x': jax.random.normal(k1, (B, L, D), dtype=jnp.float32), 'in_proj_w': jax.random.normal(k2, (3 * D, D), dtype=jnp.float32) * scale, 'in_proj_b': jnp.zeros((3 * D,), dtype=jnp.float32), 'out_w': jax.random.normal(k3, (D, D), dtype=jnp.float32) * scale, 'out_b': jnp.zeros((D,), dtype=jnp.float32)}
    _L2_attn_in = _L2_attn_setup()

    def _L2_ffn_setup():
        import jax, jax.numpy as jnp
        import numpy as np
        B, S, H = (2, 128, 128)
        E, I = (16, 64)
        TOP_K = 2
        N_SHARED = 2
        SCALE = 1.0
        IS = I * N_SHARED
        key = jax.random.key(seed)
        ks = jax.random.split(key, 8)
        sd = 0.02
        return {'hidden_states': jax.random.normal(ks[0], (B, S, H), jnp.float32), 'gate_w': jax.random.normal(ks[1], (E, H), jnp.float32) * sd, 'w_gate': jax.random.normal(ks[2], (E, H, I), jnp.float32) * sd, 'w_up': jax.random.normal(ks[3], (E, H, I), jnp.float32) * sd, 'w_down': jax.random.normal(ks[4], (E, I, H), jnp.float32) * sd, 'ws_gate': jax.random.normal(ks[5], (H, IS), jnp.float32) * sd, 'ws_up': jax.random.normal(ks[6], (H, IS), jnp.float32) * sd, 'ws_down': jax.random.normal(ks[7], (IS, H), jnp.float32) * sd}
    _L2_ffn_in = _L2_ffn_setup()

    def _L3_attn_setup():
        import jax, jax.numpy as jnp
        import numpy as np
        B, T, D, S = (8, 512, 128, 128)
        EPS = 1e-05

        def _gla(x, Wq, bq, Wk, bk, Wv, bv, Wg, bg, Wo, bo, gamma, beta):
            q = x @ Wq + bq
            k = x @ Wk + bk
            v = x @ Wv + bv
            g = jax.nn.sigmoid(x @ Wg + bg)

            def step(state, qkvg):
                qt, kt, vt, gt = qkvg
                state = gt[:, :, None] * state + kt[:, :, None] * vt[:, None, :]
                out = jnp.einsum('bs,bst->bt', qt, state)
                return (state, out)
            init = jnp.zeros((x.shape[0], Wq.shape[1], Wq.shape[1]), x.dtype)
            seq = (q.transpose(1, 0, 2), k.transpose(1, 0, 2), v.transpose(1, 0, 2), g.transpose(1, 0, 2))
            _, outs = jax.lax.scan(step, init, seq)
            out = outs.transpose(1, 0, 2)
            y = x + out @ Wo + bo
            mu = jnp.mean(y, axis=-1, keepdims=True)
            var = jnp.mean(jnp.square(y - mu), axis=-1, keepdims=True)
            return (y - mu) * jax.lax.rsqrt(var + EPS) * gamma + beta
        key = jax.random.key(seed)
        ks = jax.random.split(key, 12)
        sD = 1.0 / np.sqrt(D)
        sS = 1.0 / np.sqrt(S)
        return {'x': jax.random.normal(ks[0], (B, T, D), jnp.float32), 'Wq': jax.random.normal(ks[1], (D, S), jnp.float32) * sD, 'bq': jnp.zeros((S,), jnp.float32), 'Wk': jax.random.normal(ks[2], (D, S), jnp.float32) * sD, 'bk': jnp.zeros((S,), jnp.float32), 'Wv': jax.random.normal(ks[3], (D, S), jnp.float32) * sD, 'bv': jnp.zeros((S,), jnp.float32), 'Wg': jax.random.normal(ks[4], (D, S), jnp.float32) * sD, 'bg': jnp.zeros((S,), jnp.float32), 'Wo': jax.random.normal(ks[5], (S, D), jnp.float32) * sS, 'bo': jnp.zeros((D,), jnp.float32), 'gamma': jnp.ones((D,), jnp.float32), 'beta': jnp.zeros((D,), jnp.float32)}
    _L3_attn_in = _L3_attn_setup()

    def _L3_ffn_setup():
        import jax, jax.numpy as jnp
        import numpy as np
        NUM_EXPERTS = 8
        TOP_K = 2
        MOE_DIM = 256

        def _moe_forward(x, moe_router, moe_w13, moe_w2):
            b, s, d = x.shape
            x_flat = x.reshape(b * s, d)
            router_logits = jnp.einsum('td,de->te', x_flat, moe_router)
            topk_logits, topk_idx = jax.lax.top_k(router_logits, TOP_K)
            topk_weights = jax.nn.softmax(topk_logits, axis=-1).astype(x.dtype)
            tokens = x_flat.shape[0]
            expert_ids = topk_idx.reshape(tokens * TOP_K)
            dispatch_weights = topk_weights.reshape(tokens * TOP_K)
            sort_idx = jnp.argsort(expert_ids, axis=0)
            token_ids = jnp.arange(tokens * TOP_K, dtype=jnp.int32) // TOP_K
            token_ids_sort = token_ids[sort_idx]
            x_sort = x_flat[token_ids_sort]
            w_sort = dispatch_weights[sort_idx].astype(x_flat.dtype)
            group_sizes = jnp.bincount(expert_ids, length=NUM_EXPERTS).astype(jnp.int32)
            w13_out = jax.lax.ragged_dot(x_sort, moe_w13, group_sizes)
            gate, up = jnp.split(w13_out, [MOE_DIM], axis=-1)
            hidden = jax.nn.silu(gate) * up
            out_dispatch = jax.lax.ragged_dot(hidden, moe_w2, group_sizes)
            out_flat = jnp.zeros_like(x_flat).at[token_ids_sort].add(out_dispatch * w_sort[:, None], mode='drop')
            return out_flat.reshape(b, s, d)
        key = jax.random.key(seed)
        k1, k2, k3, k4 = jax.random.split(key, 4)
        B, S, D = (4, 256, 128)
        x = jax.random.normal(k1, (B, S, D), dtype=jnp.float32)
        moe_router = jax.random.normal(k2, (D, NUM_EXPERTS), dtype=jnp.float32) * 0.02
        moe_w13 = jax.random.normal(k3, (NUM_EXPERTS, D, 2 * MOE_DIM), dtype=jnp.float32) * 0.02
        moe_w2 = jax.random.normal(k4, (NUM_EXPERTS, MOE_DIM, D), dtype=jnp.float32) * 0.02
        return {'x': x, 'moe_router': moe_router, 'moe_w13': moe_w13, 'moe_w2': moe_w2}
    _L3_ffn_in = _L3_ffn_setup()
    _d = {'L0_attn_x': _L0_attn_in['x'], 'L0_attn_A': _L0_attn_in['A'], 'L0_attn_Bw': _L0_attn_in['Bw'], 'L0_attn_Bb': _L0_attn_in['Bb'], 'L0_attn_Cw': _L0_attn_in['Cw'], 'L0_attn_Cb': _L0_attn_in['Cb'], 'L0_attn_Dw': _L0_attn_in['Dw'], 'L0_attn_Db': _L0_attn_in['Db'], 'L0_attn_W_ih': _L0_attn_in['W_ih'], 'L0_attn_b_ih': _L0_attn_in['b_ih'], 'L0_attn_W_hh': _L0_attn_in['W_hh'], 'L0_attn_b_hh': _L0_attn_in['b_hh'], 'L0_attn_proj_w': _L0_attn_in['proj_w'], 'L0_attn_proj_b': _L0_attn_in['proj_b'], 'L0_attn_gate_w': _L0_attn_in['gate_w'], 'L0_attn_gate_b': _L0_attn_in['gate_b'], 'L0_ffn_W1': _L0_ffn_in['W1'], 'L0_ffn_b1': _L0_ffn_in['b1'], 'L0_ffn_quantum_phases': _L0_ffn_in['quantum_phases'], 'L0_ffn_quantum_weights_real': _L0_ffn_in['quantum_weights_real'], 'L0_ffn_quantum_weights_imag': _L0_ffn_in['quantum_weights_imag'], 'L0_ffn_W2': _L0_ffn_in['W2'], 'L0_ffn_b2': _L0_ffn_in['b2'], 'L1_attn_Wq': _L1_attn_in['Wq'], 'L1_attn_Wk': _L1_attn_in['Wk'], 'L1_attn_Wv': _L1_attn_in['Wv'], 'L1_attn_Wg': _L1_attn_in['Wg'], 'L1_attn_Wgk': _L1_attn_in['Wgk'], 'L1_attn_bgk': _L1_attn_in['bgk'], 'L1_attn_Wo': _L1_attn_in['Wo'], 'L1_attn_gnorm_w': _L1_attn_in['gnorm_w'], 'L1_ffn_gate_w': _L1_ffn_in['gate_w'], 'L1_ffn_gate_b': _L1_ffn_in['gate_b'], 'L1_ffn_W1': _L1_ffn_in['W1'], 'L1_ffn_b1': _L1_ffn_in['b1'], 'L1_ffn_W2': _L1_ffn_in['W2'], 'L1_ffn_b2': _L1_ffn_in['b2'], 'L2_attn_in_proj_w': _L2_attn_in['in_proj_w'], 'L2_attn_in_proj_b': _L2_attn_in['in_proj_b'], 'L2_attn_out_w': _L2_attn_in['out_w'], 'L2_attn_out_b': _L2_attn_in['out_b'], 'L2_ffn_gate_w': _L2_ffn_in['gate_w'], 'L2_ffn_w_gate': _L2_ffn_in['w_gate'], 'L2_ffn_w_up': _L2_ffn_in['w_up'], 'L2_ffn_w_down': _L2_ffn_in['w_down'], 'L2_ffn_ws_gate': _L2_ffn_in['ws_gate'], 'L2_ffn_ws_up': _L2_ffn_in['ws_up'], 'L2_ffn_ws_down': _L2_ffn_in['ws_down'], 'L3_attn_Wq': _L3_attn_in['Wq'], 'L3_attn_bq': _L3_attn_in['bq'], 'L3_attn_Wk': _L3_attn_in['Wk'], 'L3_attn_bk': _L3_attn_in['bk'], 'L3_attn_Wv': _L3_attn_in['Wv'], 'L3_attn_bv': _L3_attn_in['bv'], 'L3_attn_Wg': _L3_attn_in['Wg'], 'L3_attn_bg': _L3_attn_in['bg'], 'L3_attn_Wo': _L3_attn_in['Wo'], 'L3_attn_bo': _L3_attn_in['bo'], 'L3_attn_gamma': _L3_attn_in['gamma'], 'L3_attn_beta': _L3_attn_in['beta'], 'L3_ffn_moe_router': _L3_ffn_in['moe_router'], 'L3_ffn_moe_w13': _L3_ffn_in['moe_w13'], 'L3_ffn_moe_w2': _L3_ffn_in['moe_w2']}
    _x0 = _d['L0_attn_x']
    _d['L0_attn_x'] = jax.random.normal(jax.random.fold_in(jax.random.key(seed), 1), (32, 256, 128), dtype=_x0.dtype)
    del _x0
    return _d

def reference(L0_attn_x, L0_attn_A, L0_attn_Bw, L0_attn_Bb, L0_attn_Cw, L0_attn_Cb, L0_attn_Dw, L0_attn_Db, L0_attn_W_ih, L0_attn_b_ih, L0_attn_W_hh, L0_attn_b_hh, L0_attn_proj_w, L0_attn_proj_b, L0_attn_gate_w, L0_attn_gate_b, L0_ffn_W1, L0_ffn_b1, L0_ffn_quantum_phases, L0_ffn_quantum_weights_real, L0_ffn_quantum_weights_imag, L0_ffn_W2, L0_ffn_b2, L1_attn_Wq, L1_attn_Wk, L1_attn_Wv, L1_attn_Wg, L1_attn_Wgk, L1_attn_bgk, L1_attn_Wo, L1_attn_gnorm_w, L1_ffn_gate_w, L1_ffn_gate_b, L1_ffn_W1, L1_ffn_b1, L1_ffn_W2, L1_ffn_b2, L2_attn_in_proj_w, L2_attn_in_proj_b, L2_attn_out_w, L2_attn_out_b, L2_ffn_gate_w, L2_ffn_w_gate, L2_ffn_w_up, L2_ffn_w_down, L2_ffn_ws_gate, L2_ffn_ws_up, L2_ffn_ws_down, L3_attn_Wq, L3_attn_bq, L3_attn_Wk, L3_attn_bk, L3_attn_Wv, L3_attn_bv, L3_attn_Wg, L3_attn_bg, L3_attn_Wo, L3_attn_bo, L3_attn_gamma, L3_attn_beta, L3_ffn_moe_router, L3_ffn_moe_w13, L3_ffn_moe_w2):

    def _L0_attn_ref(x, A, Bw, Bb, Cw, Cb, Dw, Db, W_ih, b_ih, W_hh, b_hh, proj_w, proj_b, gate_w, gate_b):
        import jax, jax.numpy as jnp
        import numpy as np
        DIM, SSM, RNN = (128, 64, 128)
        B, N, D = x.shape
        R = W_hh.shape[1]
        bx = jnp.einsum('bnd,sd->bns', x, Bw) + Bb
        dx = jnp.einsum('bnd,ed->bne', x, Dw) + Db
        gx = jax.nn.sigmoid(jnp.einsum('bnd,gd->bng', x, gate_w) + gate_b)
        ih = jnp.einsum('bnd,rd->bnr', x, W_ih) + b_ih
        bx_t = jnp.swapaxes(bx, 0, 1)
        dx_t = jnp.swapaxes(dx, 0, 1)
        gx_t = jnp.swapaxes(gx, 0, 1)
        ih_t = jnp.swapaxes(ih, 0, 1)
        h_ssm0 = jnp.zeros((B, A.shape[0]), x.dtype)
        h_rnn0 = jnp.zeros((B, R), x.dtype)

        def step(carry, inp):
            h_ssm, h_rnn = carry
            bxt, dxt, gxt, iht = inp
            h_ssm = jax.nn.silu(h_ssm @ A.T + bxt)
            y_ssm = h_ssm @ Cw.T + Cb + dxt
            hh = h_rnn @ W_hh.T + b_hh
            i_r, i_z, i_n = jnp.split(iht, 3, axis=-1)
            h_r, h_z, h_n = jnp.split(hh, 3, axis=-1)
            r = jax.nn.sigmoid(i_r + h_r)
            z = jax.nn.sigmoid(i_z + h_z)
            n = jnp.tanh(i_n + r * h_n)
            h_rnn = (1.0 - z) * n + z * h_rnn
            y_rnn = h_rnn @ proj_w.T + proj_b
            fused = gxt[:, :1] * y_ssm + gxt[:, 1:2] * y_rnn
            return ((h_ssm, h_rnn), fused)
        _, out = jax.lax.scan(step, (h_ssm0, h_rnn0), (bx_t, dx_t, gx_t, ih_t))
        return jnp.swapaxes(out, 0, 1)

    def _L0_ffn_ref(x, W1, b1, quantum_phases, quantum_weights_real, quantum_weights_imag, W2, b2):
        import jax, jax.numpy as jnp
        import numpy as np
        B, S, D_MODEL, D_FF = (4, 256, 128, 512)

        def _quantum_transform(hidden, theta, w_real, w_imag):
            imag = w_imag * jnp.sin(theta + hidden * 0.1)
            quantum_phase = jnp.cos(theta) * w_real + jnp.sin(theta) * w_imag
            return hidden + quantum_phase * imag * 0.1
        hidden = jnp.einsum('bsd,df->bsf', x, W1) + b1
        q = _quantum_transform(hidden, quantum_phases, quantum_weights_real, quantum_weights_imag)
        act = jax.nn.relu(q)
        return jnp.einsum('bsf,fd->bsd', act, W2) + b2

    def _L1_attn_ref(x, Wq, Wk, Wv, Wg, Wgk, bgk, Wo, gnorm_w):
        import jax, jax.numpy as jnp
        import numpy as np
        HID = 128
        NH = 4
        DK = 32
        DV = 64
        C = 64
        EPS = 1e-05
        GLN = 16.0

        def _xavier(key, shape, gain=2 ** (-2.5)):
            fan_in, fan_out = shape
            lim = gain * np.sqrt(6.0 / (fan_in + fan_out))
            return jax.random.uniform(key, shape, jnp.float32, -lim, lim)

        def _chunk_simple_gla(q, k, v, g):
            B, H, N, dk = q.shape
            dv = v.shape[-1]
            nc = N // C
            scale = dk ** (-0.5)
            q = q.reshape(B, H, nc, C, dk) * scale
            k = k.reshape(B, H, nc, C, dk)
            v = v.reshape(B, H, nc, C, dv)
            g = g.reshape(B, H, nc, C)
            gc = jnp.cumsum(g, axis=-1)
            gt = gc[..., -1]
            dec = gc[..., :, None] - gc[..., None, :]
            mask = jnp.tril(jnp.ones((C, C), bool))
            A = jnp.einsum('bhntd,bhnsd->bhnts', q, k)
            A = A * jnp.where(mask, jnp.exp(jnp.where(mask, dec, 0.0)), 0.0)
            o_intra = jnp.einsum('bhnts,bhnsd->bhntd', A, v)
            qs = jnp.moveaxis(q, 2, 0)
            ks_ = jnp.moveaxis(k, 2, 0)
            vs = jnp.moveaxis(v, 2, 0)
            gcs = jnp.moveaxis(gc, 2, 0)
            gts = jnp.moveaxis(gt, 2, 0)
            S0 = jnp.zeros((B, H, dk, dv), q.dtype)

            def step(S, inp):
                qc, kc, vc, gcc, gtc = inp
                o_int = jnp.einsum('bhtd,bhde->bhte', qc * jnp.exp(gcc)[..., None], S)
                kd = kc * jnp.exp(gtc[..., None] - gcc)[..., None]
                S = jnp.exp(gtc)[..., None, None] * S + jnp.einsum('bhtd,bhte->bhde', kd, vc)
                return (S, o_int)
            _, o_inter = jax.lax.scan(step, S0, (qs, ks_, vs, gcs, gts))
            o = o_intra + jnp.moveaxis(o_inter, 0, 2)
            return o.reshape(B, H, N, dv)
        B, N, _ = x.shape
        q = (x @ Wq).reshape(B, N, NH, DK).transpose(0, 2, 1, 3)
        k = (x @ Wk).reshape(B, N, NH, DK).transpose(0, 2, 1, 3)
        v = (x @ Wv).reshape(B, N, NH, DV).transpose(0, 2, 1, 3)
        gk = (x @ Wgk + bgk).transpose(0, 2, 1)
        gk = jax.nn.log_sigmoid(gk) / GLN
        o = _chunk_simple_gla(q, k, v, gk)
        o = o.transpose(0, 2, 1, 3)
        g = (x @ Wg).reshape(B, N, NH, DV)
        on = o * jax.lax.rsqrt(jnp.mean(o * o, axis=-1, keepdims=True) + EPS) * gnorm_w
        o = on * (g * jax.nn.sigmoid(g))
        o = o.reshape(B, N, NH * DV)
        return o @ Wo

    def _L1_ffn_ref(x, gate_w, gate_b, W1, b1, W2, b2):
        import jax, jax.numpy as jnp
        import numpy as np
        NUM_EXPERTS = 8
        TOP_K = 2
        B, S, D = x.shape
        xf = x.reshape(-1, D)
        gate_logits = xf @ gate_w + gate_b
        top_vals, top_idx = jax.lax.top_k(gate_logits, TOP_K)
        top_w = jax.nn.softmax(top_vals, axis=-1)
        dense_w = jnp.sum(jax.nn.one_hot(top_idx, NUM_EXPERTS, dtype=top_w.dtype) * top_w[..., None], axis=1)

        def body(acc, params):
            W1e, b1e, W2e, b2e, we = params
            h = jax.nn.silu(xf @ W1e + b1e)
            y = h @ W2e + b2e
            return (acc + we[:, None] * y, None)
        out0 = jnp.zeros_like(xf)
        out, _ = jax.lax.scan(body, out0, (W1, b1, W2, b2, dense_w.T))
        return out.reshape(B, S, D)

    def _L2_attn_ref(x, in_proj_w, in_proj_b, out_w, out_b):
        import jax, jax.numpy as jnp
        import numpy as np
        WINDOW = 64
        SHIFT = 32
        HEADS = 8
        B, L, D = x.shape
        H, W, S = (HEADS, WINDOW, SHIFT)
        hd = D // H
        xs = jnp.roll(x, -S, axis=1)
        nw = L // W
        xw = xs.reshape(B * nw, W, D)
        qkv = xw @ in_proj_w.T + in_proj_b
        q, k, v = jnp.split(qkv, 3, axis=-1)

        def to_heads(t):
            return t.reshape(-1, W, H, hd).transpose(0, 2, 1, 3)
        q, k, v = (to_heads(q), to_heads(k), to_heads(v))
        scores = jnp.einsum('nhqd,nhkd->nhqk', q, k) * (1.0 / np.sqrt(hd))
        attn = jax.nn.softmax(scores, axis=-1)
        o = jnp.einsum('nhqk,nhkd->nhqd', attn, v)
        o = o.transpose(0, 2, 1, 3).reshape(-1, W, D)
        o = o @ out_w.T + out_b
        o = o.reshape(B, L, D)
        o = jnp.roll(o, S, axis=1)
        return o + o

    def _L2_ffn_ref(hidden_states, gate_w, w_gate, w_up, w_down, ws_gate, ws_up, ws_down):
        import jax, jax.numpy as jnp
        import numpy as np
        B, S, H = (2, 128, 128)
        E, I = (16, 64)
        TOP_K = 2
        N_SHARED = 2
        SCALE = 1.0
        IS = I * N_SHARED
        b, s, h = hidden_states.shape
        x = hidden_states.reshape(-1, h)
        T = x.shape[0]
        logits = jnp.einsum('th,eh->te', x.astype(jnp.float32), gate_w.astype(jnp.float32))
        scores = jax.nn.softmax(logits, axis=-1)
        topk_w, topk_idx = jax.lax.top_k(scores, TOP_K)
        topk_w = topk_w * SCALE
        combine = jnp.zeros((T, E), jnp.float32).at[jnp.arange(T)[:, None], topk_idx].add(topk_w)
        g = jnp.einsum('th,ehi->tei', x, w_gate)
        u = jnp.einsum('th,ehi->tei', x, w_up)
        act = jax.nn.silu(g) * u
        routed = jnp.einsum('tei,eih,te->th', act, w_down, combine)
        sg = jax.nn.silu(x @ ws_gate) * (x @ ws_up)
        shared = sg @ ws_down
        return (routed + shared).reshape(b, s, h)

    def _L3_attn_ref(x, Wq, bq, Wk, bk, Wv, bv, Wg, bg, Wo, bo, gamma, beta):
        import jax, jax.numpy as jnp
        import numpy as np
        B, T, D, S = (8, 512, 128, 128)
        EPS = 1e-05

        def _gla(x, Wq, bq, Wk, bk, Wv, bv, Wg, bg, Wo, bo, gamma, beta):
            q = x @ Wq + bq
            k = x @ Wk + bk
            v = x @ Wv + bv
            g = jax.nn.sigmoid(x @ Wg + bg)

            def step(state, qkvg):
                qt, kt, vt, gt = qkvg
                state = gt[:, :, None] * state + kt[:, :, None] * vt[:, None, :]
                out = jnp.einsum('bs,bst->bt', qt, state)
                return (state, out)
            init = jnp.zeros((x.shape[0], Wq.shape[1], Wq.shape[1]), x.dtype)
            seq = (q.transpose(1, 0, 2), k.transpose(1, 0, 2), v.transpose(1, 0, 2), g.transpose(1, 0, 2))
            _, outs = jax.lax.scan(step, init, seq)
            out = outs.transpose(1, 0, 2)
            y = x + out @ Wo + bo
            mu = jnp.mean(y, axis=-1, keepdims=True)
            var = jnp.mean(jnp.square(y - mu), axis=-1, keepdims=True)
            return (y - mu) * jax.lax.rsqrt(var + EPS) * gamma + beta
        return _gla(x, Wq, bq, Wk, bk, Wv, bv, Wg, bg, Wo, bo, gamma, beta)

    def _L3_ffn_ref(x, moe_router, moe_w13, moe_w2):
        import jax, jax.numpy as jnp
        import numpy as np
        NUM_EXPERTS = 8
        TOP_K = 2
        MOE_DIM = 256

        def _moe_forward(x, moe_router, moe_w13, moe_w2):
            b, s, d = x.shape
            x_flat = x.reshape(b * s, d)
            router_logits = jnp.einsum('td,de->te', x_flat, moe_router)
            topk_logits, topk_idx = jax.lax.top_k(router_logits, TOP_K)
            topk_weights = jax.nn.softmax(topk_logits, axis=-1).astype(x.dtype)
            tokens = x_flat.shape[0]
            expert_ids = topk_idx.reshape(tokens * TOP_K)
            dispatch_weights = topk_weights.reshape(tokens * TOP_K)
            sort_idx = jnp.argsort(expert_ids, axis=0)
            token_ids = jnp.arange(tokens * TOP_K, dtype=jnp.int32) // TOP_K
            token_ids_sort = token_ids[sort_idx]
            x_sort = x_flat[token_ids_sort]
            w_sort = dispatch_weights[sort_idx].astype(x_flat.dtype)
            group_sizes = jnp.bincount(expert_ids, length=NUM_EXPERTS).astype(jnp.int32)
            w13_out = jax.lax.ragged_dot(x_sort, moe_w13, group_sizes)
            gate, up = jnp.split(w13_out, [MOE_DIM], axis=-1)
            hidden = jax.nn.silu(gate) * up
            out_dispatch = jax.lax.ragged_dot(hidden, moe_w2, group_sizes)
            out_flat = jnp.zeros_like(x_flat).at[token_ids_sort].add(out_dispatch * w_sort[:, None], mode='drop')
            return out_flat.reshape(b, s, d)
        return _moe_forward(x, moe_router, moe_w13, moe_w2)
    x = L0_attn_x
    x = x + 0.5 * _L0_ffn_ref(_layernorm(x, axis=-1), L0_ffn_W1, L0_ffn_b1, L0_ffn_quantum_phases, L0_ffn_quantum_weights_real, L0_ffn_quantum_weights_imag, L0_ffn_W2, L0_ffn_b2)
    x = x + _L0_attn_ref(_layernorm(x, axis=-1), L0_attn_A, L0_attn_Bw, L0_attn_Bb, L0_attn_Cw, L0_attn_Cb, L0_attn_Dw, L0_attn_Db, L0_attn_W_ih, L0_attn_b_ih, L0_attn_W_hh, L0_attn_b_hh, L0_attn_proj_w, L0_attn_proj_b, L0_attn_gate_w, L0_attn_gate_b)
    x = x + 0.5 * _L0_ffn_ref(_layernorm(x, axis=-1), L0_ffn_W1, L0_ffn_b1, L0_ffn_quantum_phases, L0_ffn_quantum_weights_real, L0_ffn_quantum_weights_imag, L0_ffn_W2, L0_ffn_b2)
    x = x + 0.5 * _L1_ffn_ref(_layernorm(x, axis=-1), L1_ffn_gate_w, L1_ffn_gate_b, L1_ffn_W1, L1_ffn_b1, L1_ffn_W2, L1_ffn_b2)
    x = x + _L1_attn_ref(_layernorm(x, axis=-1), L1_attn_Wq, L1_attn_Wk, L1_attn_Wv, L1_attn_Wg, L1_attn_Wgk, L1_attn_bgk, L1_attn_Wo, L1_attn_gnorm_w)
    x = x + 0.5 * _L1_ffn_ref(_layernorm(x, axis=-1), L1_ffn_gate_w, L1_ffn_gate_b, L1_ffn_W1, L1_ffn_b1, L1_ffn_W2, L1_ffn_b2)
    x = x + 0.5 * _L2_ffn_ref(_layernorm(x, axis=-1), L2_ffn_gate_w, L2_ffn_w_gate, L2_ffn_w_up, L2_ffn_w_down, L2_ffn_ws_gate, L2_ffn_ws_up, L2_ffn_ws_down)
    x = x + _L2_attn_ref(_layernorm(x, axis=-1), L2_attn_in_proj_w, L2_attn_in_proj_b, L2_attn_out_w, L2_attn_out_b)
    x = x + 0.5 * _L2_ffn_ref(_layernorm(x, axis=-1), L2_ffn_gate_w, L2_ffn_w_gate, L2_ffn_w_up, L2_ffn_w_down, L2_ffn_ws_gate, L2_ffn_ws_up, L2_ffn_ws_down)
    x = x + 0.5 * _L3_ffn_ref(_layernorm(x, axis=-1), L3_ffn_moe_router, L3_ffn_moe_w13, L3_ffn_moe_w2)
    x = x + _L3_attn_ref(_layernorm(x, axis=-1), L3_attn_Wq, L3_attn_bq, L3_attn_Wk, L3_attn_bk, L3_attn_Wv, L3_attn_bv, L3_attn_Wg, L3_attn_bg, L3_attn_Wo, L3_attn_bo, L3_attn_gamma, L3_attn_beta)
    x = x + 0.5 * _L3_ffn_ref(_layernorm(x, axis=-1), L3_ffn_moe_router, L3_ffn_moe_w13, L3_ffn_moe_w2)
    return x

_drawn_inputs = setup_inputs


def setup_inputs(seed=0):
    import zlib

    import numpy as np

    out = dict(_drawn_inputs(seed))
    spreads = {'L0_attn_Bb': (0.0, 0.8),
     'L0_attn_Cb': (0.0, 0.1),
     'L0_attn_Db': (0.0, 0.1),
     'L0_attn_b_ih': (0.0, 0.473),
     'L0_attn_b_hh': (0.0, 0.8),
     'L0_attn_proj_b': (0.0, 0.1),
     'L0_attn_gate_b': (0.0, 0.8),
     'L0_ffn_b1': (0.0, 0.1),
     'L0_ffn_b2': (0.0, 0.1),
     'L1_attn_bgk': (0.0, 0.8),
     'L1_attn_gnorm_w': (1.0, 0.6),
     'L1_ffn_gate_b': (0.0, 0.1),
     'L1_ffn_b1': (0.0, 0.372),
     'L1_ffn_b2': (0.0, 0.1),
     'L2_attn_in_proj_b': (0.0, 0.1),
     'L2_attn_out_b': (0.0, 0.1),
     'L3_attn_bq': (0.0, 0.1),
     'L3_attn_bk': (0.0, 0.1),
     'L3_attn_bv': (0.0, 0.1),
     'L3_attn_bg': (0.0, 0.283),
     'L3_attn_bo': (0.0, 0.8),
     'L3_attn_gamma': (1.0, 0.2),
     'L3_attn_beta': (0.0, 0.1)}
    factors = {'L0_attn_A': 8.0,
     'L0_attn_Bw': 4.21,
     'L0_attn_Cw': 3.808,
     'L0_attn_W_hh': 8.0,
     'L0_ffn_quantum_phases': 8.0,
     'L0_ffn_quantum_weights_real': 8.0,
     'L0_ffn_quantum_weights_imag': 8.0,
     'L1_attn_Wq': 3.002,
     'L1_attn_Wk': 2.86,
     'L1_attn_Wv': 2.945,
     'L1_attn_Wg': 2.918,
     'L1_attn_Wgk': 8.0,
     'L1_attn_Wo': 2.934,
     'L2_ffn_gate_w': 8.0,
     'L2_ffn_w_gate': 8.0,
     'L2_ffn_w_up': 8.0,
     'L2_ffn_w_down': 8.0,
     'L2_ffn_ws_gate': 8.0,
     'L2_ffn_ws_up': 8.0,
     'L2_ffn_ws_down': 8.0,
     'L3_ffn_moe_router': 8.0,
     'L3_ffn_moe_w13': 8.0,
     'L3_ffn_moe_w2': 8.0}
    for name, (base, spread) in spreads.items():
        noise = np.random.default_rng([zlib.crc32(name.encode()), seed]).standard_normal(out[name].shape)
        drawn = base * np.exp(spread * noise) if base else spread * noise
        out[name] = jnp.asarray(drawn.astype(out[name].dtype))
    for name, factor in factors.items():
        out[name] = (out[name] * factor).astype(out[name].dtype)
    return out
```

```python
import math
from contextlib import ExitStack, contextmanager

import numpy as np
import concourse.bass as bass
from concourse import mybir

ALU = mybir.AluOpType
ACT = mybir.ActivationFunctionType
F32 = mybir.dt.float32
BF16 = mybir.dt.bfloat16
I32 = mybir.dt.int32
F32R = mybir.dt.float32r
AX_X = mybir.AxisListType.X

P = 128
D = 128
TILE = 512
SEQ = 256
EPS = 1e-5
LOWEST = -3.0e38


def super_steps(eng, steps, body):
    body(0, True, False)
    with eng.Fori(1, steps - 1) as s:
        body(s, False, False)
    body(steps - 1, False, True)


class Moe:

    def __init__(self, experts, groups, group, up, softmax_all, gate, gate_w, gate_b=None, up_w=None, down_w=None,
                 bias=None, bias_down=None, sel=None, rev=None, at=None, margin_after=1,
                 at_update=1, lead=None, buffers=4,
                 deep=False):
        self.experts, self.groups, self.group, self.up, self.softmax_all = experts, groups, group, up, softmax_all
        self.gate, self.gate_w, self.gate_b, self.up_w, self.down_w = gate, gate_w, gate_b, up_w, down_w
        self.bias, self.bias_down, self.sel, self.rev = bias, bias_down, sel, rev
        self.at, self.margin_after, self.at_update, self.lead, self.buffers = at, margin_after, at_update, lead, buffers
        self.deep = deep
        self.units, self.weighted = len(group), sum(g is not None for g in group)


NORM_SIGNALS = ["mean_ready", "centred", "squared", "var_ready", "root_step", "root_ready", "spread_ready",
                "xn_ready"]
GUESS = 1597463007.0


def inverse_root(dv, v, y, a, step, T, done):
    def chain(ins, k):
        ins.then_inc(step, 1)
        yield
        dv.wait_ge(step, T * INVERSE_ROOT_STEPS + k + 2)

    yield from chain(dv.tensor_scalar(y.bitcast(I32), v.bitcast(I32), -0.5, GUESS, ALU.mult, ALU.add), 0)
    for n in range(3):
        yield from chain(dv.tensor_tensor(a, y, y, ALU.mult), 3 * n + 1)
        yield from chain(dv.scalar_tensor_tensor(out=a, in0=a, scalar=-0.5, in1=v, op0=ALU.mult, op1=ALU.mult), 3 * n + 2)
        last = dv.scalar_tensor_tensor(out=y, in0=a, scalar=1.5, in1=y, op0=ALU.add, op1=ALU.mult)
        if n < 2:
            yield from chain(last, 3 * n + 3)
    last.then_inc(done, 1)


INVERSE_ROOT_STEPS = 10


class Norm:

    def __init__(self, sb, ones, ident, ps, sg, N):
        self.ones, self.ident, self.ps, self.sg = ones, ident, ps[:, 0:N], sg
        self.blocks, self.rows = max(1, N // P), min(N, P)
        self.xc, self.sq = sb("xc", [P, N]), sb("sq", [P, N])
        self.v, self.y, self.a = (sb(n, [self.rows, self.blocks]) for n in ("var", "root", "root_a"))

    def mean(self, pe, cols):
        pe.matmul(self.ps, self.ones[:, :], cols, start=True, stop=True).then_inc(self.sg["mean_ready"], 1)

    def centre(self, dv, T, cols):
        dv.wait_ge(self.sg["mean_ready"], T + 1)
        dv.tensor_tensor(self.xc[:, :], cols, self.ps, ALU.subtract).then_inc(self.sg["centred"], 1)

    def centre_view(self, dv, T, cols, view):
        dv.wait_ge(self.sg["mean_ready"], T + 1)
        dv.tensor_tensor(view(self.xc), cols, view(self.ps), ALU.subtract).then_inc(self.sg["centred"], 1)

    def square(self, ac, T):
        ac.wait_ge(self.sg["centred"], T + 1)
        ac.activation(self.sq[:, :], self.xc[:, :], ACT.Square).then_inc(self.sg["squared"], 1)

    def var(self, pe, T):
        pe.wait_ge(self.sg["squared"], T + 1)
        for b in range(self.blocks):
            mm = pe.matmul(self.ps[0:self.rows, b:b + 1], self.sq[:, b * P:b * P + self.rows], self.ones[:, 0:1],
                           start=True, stop=True)
        mm.then_inc(self.sg["var_ready"], 1)

    def root(self, dv, T):
        dv.wait_ge(self.sg["var_ready"], T + 1)
        dv.tensor_scalar(self.v[:, :], self.ps[0:self.rows, 0:self.blocks], EPS, None, ALU.add)\
            .then_inc(self.sg["root_step"], 1)
        yield
        dv.wait_ge(self.sg["root_step"], T * INVERSE_ROOT_STEPS + 1)
        yield from inverse_root(dv, self.v[:, :], self.y[:, :], self.a[:, :], self.sg["root_step"], T, self.sg["root_ready"])

    def root_at_once(self, dv, T):
        for _ in self.root(dv, T):
            pass

    def spread(self, pe, T):
        pe.wait_ge(self.sg["root_ready"], T + 1)
        for b in range(self.blocks):
            mm = pe.matmul(self.ps[:, b * P:b * P + self.rows], self.y[:, b:b + 1].broadcast_to((self.rows, P)),
                           self.ident[0:self.rows, 0:self.rows], start=True, stop=True)
        mm.then_inc(self.sg["spread_ready"], 1)

    def normalise(self, dv, T, outs):
        dv.wait_ge(self.sg["spread_ready"], T + 1)
        for out, part in outs:
            last = dv.tensor_tensor(out, part(self.xc), part(self.ps), ALU.mult)
        last.then_inc(self.sg["xn_ready"], 1)


WIDE_NORM_SIGNALS = ["mean_ready", "centred", "squared", "var_ready", "std_ready", "inverted", "xn_ready"]


class WideNorm:

    def __init__(self, sb, ones, ps, sg, N):
        self.ones, self.ps, self.sg = ones, ps[:, 0:N], sg
        self.xc, self.sq, self.std, self.inv = sb("xc", [P, N]), sb("sq", [P, N]), sb("std", [P, N]), sb("inv", [P, N])

    def mean(self, pe, cols):
        pe.matmul(self.ps, self.ones[:, :], cols, start=True, stop=True).then_inc(self.sg["mean_ready"], 1)

    def centre(self, dv, T, cols):
        dv.wait_ge(self.sg["mean_ready"], T + 1)
        dv.tensor_tensor(self.xc[:, :], cols, self.ps, ALU.subtract).then_inc(self.sg["centred"], 1)

    def square(self, ac, T):
        ac.wait_ge(self.sg["centred"], T + 1)
        ac.activation(self.sq[:, :], self.xc[:, :], ACT.Square).then_inc(self.sg["squared"], 1)

    def var(self, pe, T):
        pe.wait_ge(self.sg["squared"], T + 1)
        pe.matmul(self.ps, self.ones[:, :], self.sq[:, :], start=True, stop=True).then_inc(self.sg["var_ready"], 1)

    def root(self, ac, T):
        ac.wait_ge(self.sg["var_ready"], T + 1)
        ac.activation(self.std[:, :], self.ps, ACT.Sqrt, bias=self.ones.eps[:, :]).then_inc(self.sg["std_ready"], 1)

    def normalise(self, dv, T, outs):
        dv.wait_ge(self.sg["std_ready"], T + 1)
        dv.reciprocal(self.inv[:, :], self.std[:, :]).then_inc(self.sg["inverted"], 1)
        dv.wait_ge(self.sg["inverted"], T + 1)
        for out, part in outs:
            last = dv.tensor_tensor(out, part(self.xc), part(self.inv), ALU.mult)
        last.then_inc(self.sg["xn_ready"], 1)


def whole(t):
    return t[:, :]


MOE_SIGNALS = ["xn_high_ready", "xn_low_ready", "logits_ready", "gating_step", "margin_ready", "tanh_ready", "split_step",
               "weights_ready", "parts_cleared", "weights_turned", "weights_kept", "wb_ready", "gate_ready", "up_ready",
               "silu_ready", "scaled_by_up", "hidden_ready", "high_ready", "low_ready", "down_done", "x_updated"]


def split_weights(nc, pairs, loaded, loads, tag):
    with ExitStack() as ctx:
        highs = ctx.enter_context(nc.semaphore(tag + "_highs"))
        block = ctx.enter_context(nc.Block())

        @block.sync
        def _(sp):
            for tensor, source, arrived in loads:
                sp.dma_start(every(tensor), source).then_inc(arrived, 16)

        @block.scalar
        def _(ac):
            ac.wait_ge(loaded, 16 * len(pairs))
            for w, high, low in pairs:
                ac.activation(every(high), every(w), ACT.Copy).then_inc(highs, 1)

        @block.vector
        def _(dv):
            for n, (w, high, low) in enumerate(pairs):
                dv.wait_ge(highs, n + 1)
                dv.tensor_tensor(every(low), every(w), every(high).bitcast(F32), ALU.subtract)

    with nc.Block() as block:
        @block.gpsimd
        def _(pool):
            pool.sem_clear(highs)


def every(t):
    return t[tuple(slice(None) for _ in t.shape)]


def moe_pass(nc, x, ones, ident, ident16, banks, moe, sg, NT, tag):
    E, U, W3 = moe.experts, moe.units, 3 * moe.experts
    g_ps = [banks[4], banks[5]] if moe.up else [banks[3], banks[4], banks[5], banks[6]]
    u_ps = [banks[3], banks[6]]
    wb_ps, y_ps, gt_ps = [banks[1], banks[2]], banks[7], banks[0]
    lag = 3
    NG = len(g_ps)
    deep = moe.deep
    ahead = 2 if deep else 1
    steps = 14 + (5 if not moe.softmax_all else 9)
    NB = moe.buffers
    logits_ps = gt_ps[:, 0:4 * E].rearrange("p (b e) -> p b e", b=4)
    at_mean, at_var, at_spread, at_logits, at_turn = moe.at
    first_unit = [moe.group.index(g) for g in range(moe.groups)]
    last_unit = [max(u for u in range(U) if moe.group[u] == g) for g in range(moe.groups)]

    def broadcasts_after(u):
        return [(first_unit[g] < moe.lead[g], g) for g in range(moe.groups) if (first_unit[g] - moe.lead[g]) % U == u]

    with ExitStack() as ctx:
        def sb(name, shape, dt=F32):
            return ctx.enter_context(nc.sbuf_tensor(f"{tag}_{name}", shape, dt))

        def ring(name, dt=F32):
            return [sb(f"{name}{i}", [P, TILE], dt) for i in range(NB)]

        xn = sb("xn", [P, TILE])
        xn_high, xn_low = ([sb(f"xn_{n}{i}", [P, TILE], F32R) for i in range(2)] for n in ("high", "low"))
        norm = Norm(sb, ones, ident, banks[0], sg, TILE)
        hid, high, low = ring("hid"), ring("high", F32R), ring("low", F32R)
        wts16 = [sb(f"wts16{i}", [W3, TILE], BF16) for i in range(2)]
        wts32 = [sb(f"wts32{i}", [W3, TILE], F32R) for i in range(2)] if moe.bias_down is not None else None
        lg, lg2, mk, c1, f1, f2 = (sb(n, [P, 4, E]) for n in ("lg", "lg2", "mk", "c1", "f1", "f2"))
        ex, ex2 = sb("ex", [P, 4, E]), sb("ex2", [P, 4, E])
        m1, m2, cm, dm, th, w1, w2 = (sb(n, [P, 4, 1]) for n in ("m1", "m2", "cm", "dm", "th", "w1", "w2"))
        rows = W3 if W3 <= 32 else P
        parts = sb("parts", [P, 4, rows], BF16)
        turned_ps = gt_ps[0:rows, 0:TILE // 2].bitcast(BF16)
        kept_ps = gt_ps[0:W3, 0:TILE // 2].bitcast(BF16)
        block = ctx.enter_context(nc.Block())

        def tile(t):
            return x[:, bass.ds(t * TILE, TILE)]

        def spread(v):
            return v[:, :, :].broadcast_to((P, 4, E))

        def three(pe, out, w, u, xh, xl):
            pe.matmul(out, w[0][:, u, :], xh, start=True, stop=False)
            pe.matmul(out, w[1][:, u, :], xh, start=False, stop=False)
            return pe.matmul(out, w[0][:, u, :], xl, start=False, stop=True)

        @block.tensor
        def _(pe):
            def logits(T):
                pe.wait_ge(sg["xn_ready"], T + 1)
                for b in range(4):
                    mm = pe.matmul(logits_ps[:, b, :], xn[:, b * P:(b + 1) * P], moe.gate[:, :],
                                   start=True, stop=True)
                mm.then_inc(sg["logits_ready"], 1)

            def turn(T, normed):
                if normed is not None:
                    pe.wait_ge(sg["xn_ready"], normed)
                pe.wait_ge(sg["weights_ready"], T + 1)
                for b in range(4):
                    mm = pe.transpose(turned_ps[:, b * P:(b + 1) * P], parts[:, b, :], ident16[:, :])
                mm.then_inc(sg["weights_turned"], 1)

            def broadcast(T, g, p, before):
                if g == 0:
                    pe.wait_ge(sg["weights_kept"], T + 1)
                if g >= 2:
                    pe.wait_ge(sg["hidden_ready"], T * U + last_unit[g - 2] + 1)
                elif before:
                    pe.wait_ge(sg["hidden_ready"], (T - 1) * U + last_unit[g - 2] + 1)
                pe.matmul(wb_ps[g % 2][:, :], moe.sel[:, g, :], wts16[p][:, :], start=True, stop=True)\
                    .then_inc(sg["wb_ready"], 1)

            def gate_up(T, u, p, first):
                n = p * U + u
                if moe.up and (n >= NG or not first):
                    if u >= NG and moe.group[u - NG] is None:
                        pe.wait_ge(sg["hidden_ready"], T * U + u + 1 - NG)
                    elif u < NG and moe.group[u - NG] is None:
                        pe.wait_ge(sg["hidden_ready"], T * U + u + 1 - NG)
                    elif u >= NG:
                        pe.wait_ge(sg["scaled_by_up"], T * moe.weighted + u + 1 - NG)
                    else:
                        pe.wait_ge(sg["scaled_by_up"], (T - 1) * moe.weighted + (U + u + 1 - NG))
                if u == 0:
                    pe.wait_ge(sg["xn_low_ready"], T + 1)
                three(pe, g_ps[n % NG][:, :], moe.gate_w, u, xn_high[p][:, :], xn_low[p][:, :])\
                    .then_inc(sg["gate_ready"], 1)
                if moe.up:
                    three(pe, u_ps[n % 2][:, :], moe.up_w, u, xn_high[p][:, :], xn_low[p][:, :])\
                        .then_inc(sg["up_ready"], 1)

            def down(T, u, p, before):
                n = p * U + u
                if u == 0 and before:
                    pe.wait_ge(sg["x_updated"], T)
                if u == 0 and moe.bias_down is not None:
                    for part in range(2):
                        pe.matmul(y_ps[:, :], moe.bias_down[part][:, :], wts32[p][:, :],
                                  start=(part == 0), stop=False)
                pe.wait_ge(sg["high_ready"], T * U + u + 1)
                pe.matmul(y_ps[:, :], moe.down_w[0][:, u, :], high[n % NB][:, :],
                          start=(u == 0 and moe.bias_down is None), stop=False)
                pe.matmul(y_ps[:, :], moe.down_w[1][:, u, :], high[n % NB][:, :], start=False, stop=False)
                pe.wait_ge(sg["low_ready"], T * U + u + 1)
                pe.matmul(y_ps[:, :], moe.down_w[0][:, u, :], low[n % NB][:, :], start=False, stop=(u == U - 1))\
                    .then_inc(sg["down_done"], 1)

            def body(s, first, last):
                for p in range(2):
                    t = 2 * s + p
                    T = t
                    more = not (last and p == 1)
                    norm_more = not last if deep else more
                    if first and p == 0:
                        norm.mean(pe, tile(0))
                        norm.var(pe, T)
                        norm.spread(pe, T)
                        logits(T)
                        turn(T, None)
                        if deep:
                            pe.wait_ge(sg["weights_kept"], 1)
                            norm.mean(pe, tile(1))
                            norm.var(pe, 1)
                            norm.spread(pe, 1)
                        for u in range(lag):
                            gate_up(T, u, p, True)
                        for g in range(moe.groups):
                            if first_unit[g] < moe.lead[g]:
                                broadcast(T, g, p, False)
                    for u in range(U):
                        if more and deep and u == at_logits:
                            logits(T + 1)
                        if norm_more and u == at_mean:
                            if deep:
                                pe.wait_ge(sg["gating_step"], (T + 1) * steps + 1)
                            norm.mean(pe, tile(t + ahead))
                        if norm_more and u == at_var:
                            norm.var(pe, T + ahead)
                        if norm_more and u == at_spread:
                            norm.spread(pe, T + ahead)
                        if more and not deep and u == at_logits:
                            logits(T + 1)
                        if more and u == at_turn:
                            turn(T + 1, T + ahead + 1 if deep and norm_more else None)
                        if u + lag < U:
                            gate_up(T, u + lag, p, first)
                        elif more:
                            gate_up(T + 1, u + lag - U, 1 - p, False)
                        down(T, u, p, not (first and p == 0))
                        for of_next, g in broadcasts_after(u):
                            if not of_next:
                                broadcast(T, g, p, not (first and p == 0))
                            elif more:
                                broadcast(T + 1, g, 1 - p, True)

            super_steps(pe, NT // 2, body)

        @block.scalar
        def _(ac):
            def margin(T):
                ac.wait_ge(sg["margin_ready"], T + 1)
                if moe.softmax_all:
                    ac.activation(ex[:, :, :], lg2[:, :, :], ACT.Tanh, scale=0.5).then_inc(sg["tanh_ready"], 1)
                else:
                    ac.activation(th[:, :, :], dm[:, :, :], ACT.Tanh, scale=0.5).then_inc(sg["tanh_ready"], 1)

            def keep(T, p):
                ac.wait_ge(sg["weights_turned"], T + 1)
                if moe.bias_down is not None:
                    ac.activation(wts32[p][:, :], kept_ps, ACT.Copy)
                ac.activation(wts16[p][:, :], kept_ps, ACT.Copy).then_inc(sg["weights_kept"], 1)

            def silu(T, u, p, first):
                n = p * U + u
                if n >= NB or not first:
                    ac.wait_ge(sg["low_ready"], T * U + u + 1 - NB)
                ac.wait_ge(sg["gate_ready"], T * U + u + 1)
                if moe.bias is not None:
                    ac.activation(hid[n % NB][:, :], g_ps[n % NG][:, :], ACT.Silu, bias=moe.bias[:, u:u + 1])\
                        .then_inc(sg["silu_ready"], 1)
                else:
                    ac.activation(hid[n % NB][:, :], g_ps[n % NG][:, :], ACT.Silu)\
                        .then_inc(sg["silu_ready"], 1)

            def high_part(T, u, p, first):
                n = p * U + u
                ac.wait_ge(sg["hidden_ready"], T * U + u + 1)
                if n >= NB or not first:
                    ac.wait_ge(sg["down_done"], T * U + u + 1 - NB)
                ac.activation(high[n % NB][:, :], hid[n % NB][:, :], ACT.Copy).then_inc(sg["high_ready"], 1)

            def columns_high(T, p):
                ac.wait_ge(sg["xn_ready"], T + 1)
                ac.activation(xn_high[p][:, :], xn[:, :], ACT.Copy).then_inc(sg["xn_high_ready"], 1)

            def body(s, first, last):
                for p in range(2):
                    T = 2 * s + p
                    more = not (last and p == 1)
                    norm_more = not last if deep else more
                    if first and p == 0:
                        norm.square(ac, T)
                        columns_high(T, p)
                        margin(T)
                        keep(T, p)
                        if deep:
                            norm.square(ac, 1)
                            columns_high(1, 1)
                        silu(T, 0, p, first)
                    for u in range(U):
                        if more and u == at_logits + moe.margin_after:
                            margin(T + 1)
                        if u + 1 < U:
                            silu(T, u + 1, p, first)
                        elif more:
                            silu(T + 1, 0, 1 - p, first)
                        high_part(T, u, p, first)
                        if norm_more and u == at_mean:
                            norm.square(ac, T + ahead)
                        if norm_more and u == at_spread:
                            columns_high(T + ahead, p if deep else 1 - p)
                        if more and u == at_turn:
                            keep(T + 1, 1 - p)

            super_steps(ac, NT // 2, body)

        @block.gpsimd
        def _(pool):
            def columns_low(T, p):
                pool.wait_ge(sg["xn_high_ready"], T + 1)
                pool.tensor_tensor(xn_low[p][:, :], xn[:, :], xn_high[p][:, :].bitcast(F32), ALU.subtract)\
                    .then_inc(sg["xn_low_ready"], 1)

            def low_part(T, u, p):
                n = p * U + u
                pool.wait_ge(sg["high_ready"], T * U + u + 1)
                pool.tensor_tensor(low[n % NB][:, :], hid[n % NB][:, :], high[n % NB][:, :].bitcast(F32),
                                   ALU.subtract).then_inc(sg["low_ready"], 1)

            def body(s, first, last):
                for p in range(2):
                    T = 2 * s + p
                    more = not (last and p == 1)
                    norm_more = not last if deep else more
                    if first and p == 0:
                        columns_low(T, p)
                        if deep:
                            columns_low(1, 1)
                    for u in range(U):
                        low_part(T, u, p)
                        if norm_more and u == at_spread:
                            columns_low(T + ahead, p if deep else 1 - p)

            super_steps(pool, NT // 2, body)

        @block.vector
        def _(dv):
            if rows > W3:
                dv.memset(parts[:, :, :], 0.0).then_inc(sg["parts_cleared"], 1)
                dv.wait_ge(sg["parts_cleared"], 1)

            def chain(ins, T, k):
                ins.then_inc(sg["gating_step"], 1)
                yield
                dv.wait_ge(sg["gating_step"], T * steps + k + 1)

            def choose(T):
                dv.wait_ge(sg["logits_ready"], T + 1)
                if moe.gate_b is not None:
                    yield from chain(dv.tensor_tensor(lg[:, :, :], logits_ps, moe.gate_b[:, :, :], ALU.add), T, 0)
                else:
                    yield from chain(dv.tensor_copy(lg[:, :, :], logits_ps), T, 0)
                yield from chain(dv.tensor_reduce(m1[:, :, :], lg[:, :, :], AX_X, ALU.max), T, 1)
                yield from chain(dv.tensor_tensor(mk[:, :, :], lg[:, :, :], spread(m1), ALU.is_equal), T, 2)
                yield from chain(dv.tensor_tensor(c1[:, :, :], mk[:, :, :], moe.rev[:, :, :], ALU.mult), T, 3)
                yield from chain(dv.tensor_reduce(cm[:, :, :], c1[:, :, :], AX_X, ALU.max), T, 4)
                yield from chain(dv.tensor_tensor(f1[:, :, :], c1[:, :, :], spread(cm), ALU.is_equal), T, 5)
                yield from chain(dv.scalar_tensor_tensor(out=lg2[:, :, :], in0=f1[:, :, :], scalar=LOWEST,
                                                         in1=lg[:, :, :], op0=ALU.mult, op1=ALU.add), T, 6)
                yield from chain(dv.tensor_reduce(m2[:, :, :], lg2[:, :, :], AX_X, ALU.max), T, 7)
                yield from chain(dv.tensor_tensor(mk[:, :, :], lg2[:, :, :], spread(m2), ALU.is_equal), T, 8)
                if moe.softmax_all:
                    dv.tensor_tensor(lg2[:, :, :], lg[:, :, :], spread(m1), ALU.subtract).then_inc(sg["margin_ready"], 1)
                else:
                    dv.tensor_tensor(dm[:, :, :], m2[:, :, :], m1[:, :, :], ALU.subtract).then_inc(sg["margin_ready"], 1)
                yield
                yield from chain(dv.tensor_tensor(c1[:, :, :], mk[:, :, :], moe.rev[:, :, :], ALU.mult), T, 9)
                yield from chain(dv.tensor_reduce(cm[:, :, :], c1[:, :, :], AX_X, ALU.max), T, 10)
                yield from chain(dv.tensor_tensor(f2[:, :, :], c1[:, :, :], spread(cm), ALU.is_equal), T, 11)
                dv.wait_ge(sg["tanh_ready"], T + 1)
                k = 12
                if moe.softmax_all:
                    yield from chain(dv.tensor_scalar(ex2[:, :, :], ex[:, :, :], -1.0, 1.0, ALU.mult, ALU.add), T, k)
                    yield from chain(dv.reciprocal(c1[:, :, :], ex2[:, :, :]), T, k + 1)
                    yield from chain(dv.tensor_scalar(ex[:, :, :], ex[:, :, :], 1.0, None, ALU.add), T, k + 2)
                    yield from chain(dv.tensor_tensor(ex2[:, :, :], ex[:, :, :], c1[:, :, :], ALU.mult), T, k + 3)
                    yield from chain(dv.tensor_reduce(w1[:, :, :], ex2[:, :, :], AX_X, ALU.add), T, k + 4)
                    yield from chain(dv.reciprocal(w2[:, :, :], w1[:, :, :]), T, k + 5)
                    yield from chain(dv.tensor_tensor(mk[:, :, :], f1[:, :, :], f2[:, :, :], ALU.add), T, k + 6)
                    yield from chain(dv.tensor_tensor(f1[:, :, :], ex2[:, :, :], spread(w2), ALU.mult), T, k + 7)
                    yield from chain(dv.tensor_tensor(lg[:, :, :], f1[:, :, :], mk[:, :, :], ALU.mult), T, k + 8)
                    k += 9
                else:
                    yield from chain(dv.tensor_scalar(w2[:, :, :], th[:, :, :], 0.5, 0.5, ALU.mult, ALU.add), T, k)
                    yield from chain(dv.tensor_scalar(w1[:, :, :], th[:, :, :], -0.5, 0.5, ALU.mult, ALU.add), T, k + 1)
                    yield from chain(dv.tensor_tensor(mk[:, :, :], f1[:, :, :], spread(w1), ALU.mult), T, k + 2)
                    yield from chain(dv.tensor_tensor(c1[:, :, :], f2[:, :, :], spread(w2), ALU.mult), T, k + 3)
                    yield from chain(dv.tensor_tensor(lg[:, :, :], mk[:, :, :], c1[:, :, :], ALU.add), T, k + 4)
                    k += 5
                yield from chain(dv.tensor_copy(parts[:, :, 0:E], lg[:, :, :]), T, k)
                yield from chain(dv.tensor_tensor(mk[:, :, :], lg[:, :, :], parts[:, :, 0:E], ALU.subtract), T, k + 1)
                dv.tensor_copy(parts[:, :, E:2 * E], mk[:, :, :]).then_inc(sg["split_step"], 1)
                yield
                dv.wait_ge(sg["split_step"], 2 * T + 1)
                dv.tensor_tensor(c1[:, :, :], mk[:, :, :], parts[:, :, E:2 * E], ALU.subtract)\
                    .then_inc(sg["split_step"], 1)
                yield
                dv.wait_ge(sg["split_step"], 2 * T + 2)
                dv.tensor_copy(parts[:, :, 2 * E:W3], c1[:, :, :]).then_inc(sg["weights_ready"], 1)

            def advance(small, count):
                for _ in range(count):
                    next(small, None)

            def hidden(T, u, p, root, root_count, choice, choice_count):
                n, g = p * U + u, moe.group[u]
                dv.wait_ge(sg["silu_ready"], T * U + u + 1)
                if moe.up:
                    dv.wait_ge(sg["up_ready"], T * U + u + 1)
                    if g is None:
                        dv.tensor_tensor(hid[n % NB][:, :], hid[n % NB][:, :], u_ps[n % 2][:, :], ALU.mult)\
                            .then_inc(sg["hidden_ready"], 1)
                        advance(root, root_count)
                        advance(choice, choice_count)
                        return
                    dv.tensor_tensor(hid[n % NB][:, :], hid[n % NB][:, :], u_ps[n % 2][:, :], ALU.mult)\
                        .then_inc(sg["scaled_by_up"], 1)
                    advance(root, root_count)
                    advance(choice, choice_count)
                    dv.wait_ge(sg["scaled_by_up"], T * moe.weighted + u + 1)
                dv.wait_ge(sg["wb_ready"], T * moe.groups + g + 1)
                dv.tensor_tensor(hid[n % NB][:, :], hid[n % NB][:, :], wb_ps[g % 2][:, :], ALU.mult)\
                    .then_inc(sg["hidden_ready"], 1)
                advance(root, root_count)
                advance(choice, choice_count)

            def normalise(T, before):
                if before:
                    dv.wait_ge(sg["xn_low_ready"], T)
                norm.normalise(dv, T, [(xn[:, :], whole)])

            def update(T, cols):
                dv.wait_ge(sg["down_done"], (T + 1) * U)
                dv.scalar_tensor_tensor(out=cols, in0=y_ps[:, :], scalar=0.5, in1=cols,
                                        op0=ALU.mult, op1=ALU.add).then_inc(sg["x_updated"], 1)

            def per_slot(count, start, end):
                slots = (end - start) * (2 if moe.up else 1)
                return -(-count // slots)

            def body(s, first, last):
                for p in range(2):
                    t = 2 * s + p
                    T = t
                    more = not (last and p == 1)
                    norm_more = not last if deep else more
                    if first and p == 0:
                        norm.centre(dv, T, tile(0))
                        for _ in norm.root(dv, T):
                            pass
                        normalise(T, False)
                        for _ in choose(T):
                            pass
                        if deep:
                            norm.centre(dv, 1, tile(1))
                            for _ in norm.root(dv, 1):
                                pass
                            normalise(1, True)
                    root, root_count, choice, choice_count = iter(()), 0, iter(()), 0
                    for u in range(U):
                        if norm_more and u == at_var + 1:
                            root, root_count = norm.root(dv, T + ahead), per_slot(INVERSE_ROOT_STEPS + 1, u, at_spread)
                        if more and u == at_logits + 1:
                            choice, choice_count = choose(T + 1), per_slot(steps + 4, u, at_turn)
                        hidden(T, u, p, root, root_count, choice, choice_count)
                        if u == at_spread - 1:
                            advance(root, INVERSE_ROOT_STEPS + 1)
                        if u == at_turn - 1:
                            advance(choice, steps + 4)
                        if u == moe.at_update and not (first and p == 0):
                            update(T - 1, tile(t - 1))
                        if norm_more and u == at_mean:
                            norm.centre(dv, T + ahead, tile(t + ahead))
                        if norm_more and u == at_spread:
                            normalise(T + ahead, True)
                    if last and p == 1:
                        update(T, tile(t))

            super_steps(dv, NT // 2, body)


TURNS = float(np.float32(0.1 / (2 * np.pi)))
ROUND = 1.5 * 2.0 ** 23
TWO_PI = 6.283184
FFN_SIGNALS = ["h_ready", "phase_ready", "rounded", "fraction_ready", "sine_ready", "mixed", "relu_ready",
               "down_done", "y_read", "x_updated"]


def quantum_constants(nc, w, wide, tag):
    with ExitStack() as ctx:
        F = 4

        def sb(name):
            return ctx.enter_context(nc.sbuf_tensor(f"{tag}_{name}", [P, F], F32))

        k, k2, r, r2, ta, tb, sn, cs, qp = (sb(n) for n in ("k", "k2", "r", "r2", "ta", "tb", "sn", "cs", "qp"))
        sg = ctx.enter_context(Signals(nc, tag, ["step", "reduced", "waves"]))
        step, reduced, waves = sg["step"], sg["reduced"], sg["waves"]
        block = ctx.enter_context(nc.Block())
        theta, wr, wi, b1 = w["theta"], w["wr"], w["wi"], w["b1"]

        @block.vector
        def _(dv):
            done = [0]

            def chain(ins):
                done[0] += 1
                ins.then_inc(step, 1)
                dv.wait_ge(step, done[0])

            chain(dv.tensor_scalar(k[:, :], theta[:, :], float(1 / (2 * np.pi)), ROUND, ALU.mult, ALU.add))
            chain(dv.tensor_scalar(k2[:, :], k[:, :], ROUND, None, ALU.subtract))
            chain(dv.scalar_tensor_tensor(out=r[:, :], in0=k2[:, :], scalar=-6.28125, in1=theta[:, :],
                                          op0=ALU.mult, op1=ALU.add))
            chain(dv.scalar_tensor_tensor(out=r2[:, :], in0=k2[:, :], scalar=-(2 * np.pi - 6.28125), in1=r[:, :],
                                          op0=ALU.mult, op1=ALU.add))
            chain(dv.tensor_scalar(ta[:, :], r2[:, :], float(1 / (2 * np.pi)), None, ALU.mult))
            chain(dv.scalar_tensor_tensor(out=wide["turns"][:, :], in0=b1[:, :], scalar=TURNS, in1=ta[:, :],
                                          op0=ALU.mult, op1=ALU.add))
            for shift, out in ((0.0, tb), (0.25, r)):
                chain(dv.tensor_scalar(k[:, :], ta[:, :], shift, None, ALU.add))
                chain(dv.tensor_scalar(k2[:, :], k[:, :], ROUND, None, ALU.add))
                chain(dv.scalar_tensor_tensor(out=out[:, :], in0=k2[:, :], scalar=ROUND, in1=k[:, :],
                                              op0=ALU.subtract, op1=ALU.subtract))
            dv.sem_inc(reduced, 1)
            dv.wait_ge(waves, 1)
            chain(dv.tensor_tensor(k[:, :], cs[:, :], wr[:, :], ALU.mult))
            chain(dv.tensor_tensor(k2[:, :], sn[:, :], wi[:, :], ALU.mult))
            chain(dv.tensor_tensor(qp[:, :], k[:, :], k2[:, :], ALU.add))
            chain(dv.tensor_tensor(k[:, :], qp[:, :], wi[:, :], ALU.mult))
            chain(dv.tensor_scalar(wide["factor"][:, :], k[:, :], 0.1, None, ALU.mult))
            dv.tensor_scalar(wide["half_b2"][:, :], w["b2"][:, :], 0.5, None, ALU.mult)

        @block.scalar
        def _(ac):
            ac.wait_ge(reduced, 1)
            ac.activation(sn[:, :], tb[:, :], ACT.Sin, scale=-TWO_PI)
            ac.activation(cs[:, :], r[:, :], ACT.Sin, scale=-TWO_PI).then_inc(waves, 1)


def ffn_pass(nc, x, ones, ident, banks, w, wide, sg, NT, tag):
    U, HB = 4, 4
    h_ps, v_ps, y_ps = [banks[b] for b in (1, 2, 3, 4)], [banks[5], banks[6]], banks[7]
    with ExitStack() as ctx:
        def sb(name, shape, dt=F32):
            return ctx.enter_context(nc.sbuf_tensor(f"{tag}_{name}", shape, dt))

        xn = [sb(f"xn{i}", [P, TILE]) for i in range(2)]
        norm = Norm(sb, ones, ident, banks[0], sg, TILE)
        rnd, frac, sine, mixed, hid = ([sb(f"{n}{i}", [P, TILE]) for i in range(2)]
                                       for n in ("rnd", "frac", "sine", "mixed", "hid"))
        y_sb = sb("y", [P, TILE])
        block = ctx.enter_context(nc.Block())

        def tile(t):
            return x[:, bass.ds(t * TILE, TILE)]

        class Unit:

            def __init__(self, T, p, u, first):
                self.T, self.p, self.u, self.n = T, p, u, p * U + u
                self.past = p * U + u if first else 2 * U
                self.count = T * U + u + 1

        def unit(s, p, u, first, last):
            if u < U:
                return Unit(2 * s + p, p, u, first)
            if p == 0:
                return Unit(2 * s + 1, 1, u - U, first)
            return None if last else Unit(2 * s + 2, 0, u - U, False)

        @block.tensor
        def _(pe):
            def up(i):
                if i.u == 0:
                    pe.wait_ge(sg["xn_ready"], i.T + 1)
                if i.past >= HB:
                    pe.wait_ge(sg["mixed"], i.count - HB)
                pe.matmul(h_ps[i.n % HB][:, :], w["w1"][:, i.u, :], xn[i.p][:, :], start=True, stop=True)\
                    .then_inc(sg["h_ready"], 1)

            def down(i):
                if i.u == 0 and i.past >= U:
                    pe.wait_ge(sg["y_read"], i.T)
                pe.wait_ge(sg["relu_ready"], i.count)
                pe.matmul(y_ps[:, :], w["w2"][:, i.u, :], hid[i.n % 2][:, :], start=(i.u == 0), stop=(i.u == U - 1))\
                    .then_inc(sg["down_done"], 1)

            def body(s, first, last):
                for p in range(2):
                    T = 2 * s + p
                    if first and p == 0:
                        for t in range(2):
                            if t == 1:
                                pe.wait_ge(sg["xn_ready"], 1)
                            norm.mean(pe, tile(t))
                            norm.var(pe, t)
                            norm.spread(pe, t)
                        for u in range(3):
                            up(unit(0, 0, u, True, False))
                    for u in range(U):
                        ahead = unit(s, p, u + 3, first, last)
                        if ahead:
                            up(ahead)
                        if not last and u == 0:
                            pe.wait_ge(sg["xn_ready"], T + 2)
                            norm.mean(pe, tile(T + 2))
                        if not last and u == 1:
                            norm.var(pe, T + 2)
                        down(unit(s, p, u, first, last))
                    if not last:
                        norm.spread(pe, T + 2)

            super_steps(pe, NT // 2, body)

        @block.scalar
        def _(ac):
            def phase(i):
                ac.wait_ge(sg["h_ready"], i.count)
                if i.past >= 2:
                    ac.wait_ge(sg["fraction_ready"], i.count - 2)
                ac.activation(v_ps[i.n % 2][:, :], h_ps[i.n % HB][:, :], ACT.Identity, scale=TURNS,
                              bias=wide["turns"][:, i.u:i.u + 1]).then_inc(sg["phase_ready"], 1)

            def wave(i):
                ac.wait_ge(sg["fraction_ready"], i.count)
                ac.activation(sine[i.n % 2][:, :], frac[i.n % 2][:, :], ACT.Sin, scale=-TWO_PI)\
                    .then_inc(sg["sine_ready"], 1)

            def relu(i):
                ac.wait_ge(sg["mixed"], i.count)
                if i.past >= 2:
                    ac.wait_ge(sg["down_done"], i.count - 2)
                ac.activation(hid[i.n % 2][:, :], mixed[i.n % 2][:, :], ACT.Relu, bias=w["b1"][:, i.u:i.u + 1])\
                    .then_inc(sg["relu_ready"], 1)

            def halve(T, past):
                ac.wait_ge(sg["down_done"], (T + 1) * U)
                if past:
                    ac.wait_ge(sg["x_updated"], T)
                ac.activation(y_sb[:, :], y_ps[:, :], ACT.Identity, scale=0.5, bias=wide["half_b2"][:, 0:1])\
                    .then_inc(sg["y_read"], 1)

            def body(s, first, last):
                for p in range(2):
                    T = 2 * s + p
                    if first and p == 0:
                        norm.square(ac, 0)
                        norm.square(ac, 1)
                        for u in range(2):
                            phase(unit(0, 0, u, True, False))
                        wave(unit(0, 0, 0, True, False))
                    for u in range(U):
                        later, next_one = unit(s, p, u + 2, first, last), unit(s, p, u + 1, first, last)
                        if later:
                            phase(later)
                        if next_one:
                            wave(next_one)
                        if u == 0 and not (first and p == 0):
                            halve(T - 1, not (first and p == 1))
                        relu(unit(s, p, u, first, last))
                        if not last and u == 0:
                            norm.square(ac, T + 2)
                if last:
                    halve(T, True)

            super_steps(ac, NT // 2, body)

        @block.vector
        def _(dv):
            def fraction(i):
                dv.wait_ge(sg["phase_ready"], i.count)
                dv.tensor_scalar(rnd[i.n % 2][:, :], v_ps[i.n % 2][:, :], ROUND, None, ALU.add)\
                    .then_inc(sg["rounded"], 1)
                dv.wait_ge(sg["rounded"], i.count)
                if i.past >= 2:
                    dv.wait_ge(sg["sine_ready"], i.count - 2)
                dv.scalar_tensor_tensor(out=frac[i.n % 2][:, :], in0=rnd[i.n % 2][:, :], scalar=ROUND,
                                        in1=v_ps[i.n % 2][:, :], op0=ALU.subtract, op1=ALU.subtract)\
                    .then_inc(sg["fraction_ready"], 1)

            def mix(i):
                dv.wait_ge(sg["sine_ready"], i.count)
                if i.past >= 2:
                    dv.wait_ge(sg["relu_ready"], i.count - 2)
                dv.scalar_tensor_tensor(out=mixed[i.n % 2][:, :], in0=sine[i.n % 2][:, :],
                                        scalar=wide["factor"][:, i.u:i.u + 1], in1=h_ps[i.n % HB][:, :],
                                        op0=ALU.mult, op1=ALU.add).then_inc(sg["mixed"], 1)

            def update(T):
                dv.wait_ge(sg["y_read"], T + 1)
                dv.tensor_tensor(tile(T), tile(T), y_sb[:, :], ALU.add).then_inc(sg["x_updated"], 1)

            def body(s, first, last):
                for p in range(2):
                    T = 2 * s + p
                    if first and p == 0:
                        for t in range(2):
                            norm.centre(dv, t, tile(t))
                            norm.root_at_once(dv, t)
                            norm.normalise(dv, t, [(xn[t][:, :], whole)])
                        for u in range(2):
                            fraction(unit(0, 0, u, True, False))
                        mix(unit(0, 0, 0, True, False))
                    root = iter(()) if last else norm.root(dv, T + 2)
                    for u in range(U):
                        later, next_one = unit(s, p, u + 2, first, last), unit(s, p, u + 1, first, last)
                        if later:
                            fraction(later)
                        if u >= 1:
                            for _ in range(2):
                                next(root, None)
                        if next_one:
                            mix(next_one)
                        if u >= 1:
                            for _ in range(2):
                                next(root, None)
                        if u == 1 and not (first and p == 0):
                            update(T - 1)
                        if not last and u == 0:
                            norm.centre(dv, T + 2, tile(T + 2))
                    if not last:
                        norm.normalise(dv, T + 2, [(xn[p][:, :], whole)])
                if last:
                    update(T)

            super_steps(dv, NT // 2, body)


A3_SIGNALS = ["cleared", "q_ready", "k_ready", "g_ready", "v_ready", "q_kept", "k_kept", "g_kept", "v_kept", "r_cleared",
              "p_started", "factored", "products", "pairs_ready", "placed", "o_ready", "o_kept", "y_ready", "y_kept",
              "scaled", "x_updated"]
LEVELS = 8


def channel_gla_pass(nc, x, ones, ident, banks, w, sg, sg2, NT, tag):
    BLK = TILE // P
    SEQS = TILE // SEQ
    with ExitStack() as ctx:
        def sb(name, shape, dt=F32):
            return ctx.enter_context(nc.sbuf_tensor(f"{tag}_{name}", shape, dt))

        xn = [sb(f"xn{i}", [P, TILE]) for i in range(2)]
        norm = Norm(sb, ones, ident, banks[0], sg, TILE)
        norm2 = Norm(lambda n, sh: sb(n + "2", sh), ones, ident, banks[2], sg2, TILE)
        q, k, R, PR = sb("q", [P, TILE]), sb("k", [P, TILE]), sb("R", [P, TILE]), sb("PR", [P, TILE])
        v = sb("v", [P, BLK, P])
        kt = [sb(f"kt{i}", [P, TILE]) for i in range(2)]
        qt = [sb(f"qt{i}", [P, TILE // 2]) for i in range(2)]
        near, far = sb("near", [P, TILE]), sb("far", [P, SEQS * P])
        o, y, zn, zs = sb("o", [P, TILE]), sb("y", [P, TILE]), sb("zn", [P, TILE]), sb("zs", [P, TILE])
        waiter = sb("waiter", [P, 18])
        pair_ps = [banks[5], banks[6]]
        ready = sg["cleared"]
        block = ctx.enter_context(nc.Block())

        def tile(t):
            return x[:, bass.ds(t * TILE, TILE)]

        def half(tensor, m, side):
            return tensor[:, :].rearrange("p (n two h) -> p n two h", two=2, h=1 << m)[:, :, side, :]

        def half_end(tensor, m, side):
            h = 1 << m
            n = TILE // (2 * h)
            return half(tensor, m, side)[:, :, h - 1:h].broadcast_to((P, n, h))

        def packed(tensor, m):
            return tensor[:, 0:TILE // 2].rearrange("p (n h) -> p n h", h=1 << m)

        @block.tensor
        def _(pe):
            def project(T, p):
                pe.wait_ge(sg["xn_ready"], T + 1)
                for bank, weight, signal in ((1, "wq", sg["q_ready"]), (2, "wk", sg["k_ready"]), (3, "wg", sg["g_ready"])):
                    pe.matmul(banks[bank][:, :], w[weight][:, :], xn[p][:, :], start=True, stop=True)\
                        .then_inc(signal, 1)
                for b in range(BLK):
                    mm = pe.matmul(banks[4][:, b * P:(b + 1) * P], xn[p][:, b * P:(b + 1) * P], w["wv"][:, :],
                                   start=True, stop=True)
                mm.then_inc(sg["v_ready"], 1)

            def pairs(T, c, n, before):
                out = pair_ps[n % 2]
                if before:
                    pe.wait_ge(sg["placed"], T * 9 + c - 1)
                if c == 0:
                    pe.wait_ge(sg["q_kept"], T + 1)
                    pe.wait_ge(sg["k_kept"], T + 1)
                    for b in range(BLK):
                        cut = slice(b * P, (b + 1) * P)
                        mm = pe.matmul(out[:, cut], k[:, cut], q[:, cut], start=True, stop=True)
                elif c < LEVELS:
                    left = k if c == 1 else kt[c % 2]
                    pe.wait_ge(sg["factored"], T * 8 + c)
                    for b in range(BLK):
                        mm = pe.matmul(out[:, b * 64:(b + 1) * 64], left[:, b * P:(b + 1) * P],
                                       qt[c % 2][:, b * 64:(b + 1) * 64], start=True, stop=True)
                else:
                    pe.wait_ge(sg["factored"], T * 8 + c)
                    for b in range(SEQS):
                        mm = pe.matmul(out[:, b * P:(b + 1) * P], kt[c % 2][:, b * SEQ:b * SEQ + P],
                                       qt[c % 2][:, b * P:(b + 1) * P], start=True, stop=True)
                mm.then_inc(sg["pairs_ready"], 1)

            def weigh_values(T):
                pe.wait_ge(sg["placed"], (T + 1) * 9)
                pe.wait_ge(sg["v_kept"], T + 1)
                if not isinstance(T, int) or T > 0:
                    pe.wait_ge(sg["o_kept"], T)
                for b in range(SEQS):
                    lo, hi = 2 * b * P, (2 * b + 1) * P
                    pe.matmul(banks[7][:, lo:lo + P], v[:, 2 * b, :], near[:, lo:lo + P], start=True, stop=True)
                    pe.matmul(banks[7][:, hi:hi + P], v[:, 2 * b, :], far[:, b * P:(b + 1) * P],
                              start=True, stop=False)
                    mm = pe.matmul(banks[7][:, hi:hi + P], v[:, 2 * b + 1, :], near[:, hi:hi + P],
                                   start=False, stop=True)
                mm.then_inc(sg["o_ready"], 1)

            def output(T):
                pe.wait_ge(sg["o_kept"], T + 1)
                pe.matmul(banks[1][:, :], w["wo"][:, :], o[:, :], start=True, stop=True).then_inc(sg["y_ready"], 1)

            def mean2(T):
                pe.wait_ge(sg["y_kept"], T + 1)
                norm2.mean(pe, y[:, :])

            def body(s, first, last):
                for p in range(2):
                    T = 2 * s + p
                    fresh, more = first and p == 0, not (last and p == 1)
                    if fresh:
                        norm.mean(pe, tile(0))
                        norm.var(pe, 0)
                        norm.spread(pe, 0)
                    project(T, p)
                    for c in range(9):
                        pairs(T, c, 9 * p + c, not (fresh and c < 2))
                        if not fresh and c == 1:
                            output(T - 1)
                        if not fresh and c == 3:
                            mean2(T - 1)
                        if not fresh and c == 5:
                            norm2.var(pe, T - 1)
                        if not fresh and c == 6:
                            norm2.spread(pe, T - 1)
                        if more and c == 4:
                            norm.mean(pe, tile(T + 1))
                        if more and c == 6:
                            norm.var(pe, T + 1)
                        if more and c == 7:
                            norm.spread(pe, T + 1)
                    weigh_values(T)
                if last:
                    output(T)
                    mean2(T)
                    norm2.var(pe, T)
                    norm2.spread(pe, T)

            super_steps(pe, NT // 2, body)

        @block.scalar
        def _(ac):
            def keep(T, before):
                ac.wait_ge(sg["q_ready"], T + 1)
                ac.activation(q[:, :], banks[1][:, :], ACT.Identity, bias=w["bq"][:, 0:1]).then_inc(sg["q_kept"], 1)
                ac.wait_ge(sg["k_ready"], T + 1)
                ac.activation(k[:, :], banks[2][:, :], ACT.Identity, bias=w["bk"][:, 0:1]).then_inc(sg["k_kept"], 1)
                ac.wait_ge(sg["g_ready"], T + 1)
                ac.activation(PR[:, :], banks[3][:, :], ACT.Sigmoid, bias=w["bg"][:, 0:1]).then_inc(sg["g_kept"], 1)

            def keep_o(T):
                ac.wait_ge(sg["o_ready"], T + 1)
                ac.activation(o[:, :], banks[7][:, :], ACT.Copy).then_inc(sg["o_kept"], 1)

            def body(s, first, last):
                for p in range(2):
                    T = 2 * s + p
                    fresh, more = first and p == 0, not (last and p == 1)
                    if fresh:
                        norm.square(ac, 0)
                    keep(T, not fresh)
                    if not fresh:
                        norm2.square(ac, T - 1)
                    if more:
                        norm.square(ac, T + 1)
                    keep_o(T)
                if last:
                    norm2.square(ac, T)

            super_steps(ac, NT // 2, body)

        @block.gpsimd
        def _(pool):
            for n in range(2):
                pool.memset(kt[n][:, :], 0.0)
            pool.memset(near[:, :], 0.0).then_inc(ready, 1)

            def body(s, first, last):
                for p in range(2):
                    T = 2 * s + p
                    pool.wait_ge(sg["r_cleared"], T + 1)
                    pool.wait_ge(sg["g_kept"], T + 1)
                    for m in range(LEVELS - 1):
                        pool.wait_ge(sg["factored"], T * 8 + m + 1)
                        pool.tensor_tensor(half(R, m, 0), half(R, m, 0), half_end(PR, m, 1), ALU.mult)\
                            .then_inc(sg["p_started"], 1)
                        pool.wait_ge(sg["p_started"], T * 7 + m + 1)
                        pool.tensor_tensor(half(PR, m, 1), half(PR, m, 1), half_end(PR, m, 0), ALU.mult)\
                            .then_inc(sg["products"], 1)

            super_steps(pool, NT // 2, body)

        @block.vector
        def _(dv):
            dv.wait_ge(ready, 1)

            def clear_r(T, before):
                if before:
                    dv.wait_ge(sg["products"], T * 7)
                dv.memset(R[:, :], 1.0).then_inc(sg["r_cleared"], 1)

            def keep_v(T):
                dv.wait_ge(sg["v_ready"], T + 1)
                dv.tensor_tensor(v[:, :, :], banks[4][:, :].rearrange("p (b e) -> p b e", b=BLK), w["bv"][:, :, :],
                                 ALU.add).then_inc(sg["v_kept"], 1)

            def factor(T, m, before):
                c = m + 1
                if m == 0:
                    dv.wait_ge(sg["q_kept"], T + 1)
                    dv.wait_ge(sg["k_kept"], T + 1)
                    dv.wait_ge(sg["g_kept"], T + 1)
                else:
                    dv.wait_ge(sg["products"], T * 7 + m)
                if before:
                    dv.wait_ge(sg["pairs_ready"], T * 9 + c - 1)
                if m > 0:
                    dv.tensor_tensor(half(kt[c % 2], m, 0), half(k, m, 0), half(R, m, 0), ALU.mult)
                dv.tensor_tensor(packed(qt[c % 2], m), half(q, m, 1), half(PR, m, 1), ALU.mult)\
                    .then_inc(sg["factored"], 1)

            def place(T, c, n):
                dv.wait_ge(sg["pairs_ready"], T * 9 + c + 1)
                src = pair_ps[n % 2]
                if c == 0 and not (isinstance(T, int) and T == 0):
                    dv.wait_ge(sg["o_ready"], T)
                elif 0 < c < LEVELS:
                    dv.wait_ge(sg["placed"], T * 9 + c)
                if c < LEVELS:
                    dv.memset(waiter[:, n:n + 1], 0.0)
                if c == 0:
                    ins = dv.copy_predicated(near[:, :], w["mask_diag"][:, :], src[:, :])
                elif c < LEVELS:
                    ins = dv.copy_predicated(half(near, c - 1, 1), packed(w["mask"][:, c - 1, :], c - 1),
                                             packed(src, c - 1))
                else:
                    ins = dv.tensor_copy(far[:, :], src[:, 0:SEQS * P])
                ins.then_inc(sg["placed"], 1)

            def residual(T, p):
                dv.wait_ge(sg["y_ready"], T + 1)
                dv.scalar_tensor_tensor(out=y[:, :], in0=banks[1][:, :], scalar=w["bo"][:, 0:1], in1=xn[p][:, :],
                                        op0=ALU.add, op1=ALU.add).then_inc(sg["y_kept"], 1)

            def centre2(T):
                dv.wait_ge(sg["y_kept"], T + 1)
                norm2.centre(dv, T, y[:, :])

            def finish(T):
                norm2.normalise(dv, T, [(zn[:, :], whole)])
                dv.wait_ge(sg2["xn_ready"], T + 1)
                dv.scalar_tensor_tensor(out=zs[:, :], in0=zn[:, :], scalar=w["gamma"][:, 0:1], in1=tile(T),
                                        op0=ALU.mult, op1=ALU.add).then_inc(sg["scaled"], 1)
                dv.wait_ge(sg["scaled"], T + 1)
                dv.tensor_scalar(tile(T), zs[:, :], w["beta"][:, 0:1], None, ALU.add).then_inc(sg["x_updated"], 1)

            def body(s, first, last):
                for p in range(2):
                    T = 2 * s + p
                    fresh, more = first and p == 0, not (last and p == 1)
                    if fresh:
                        norm.centre(dv, 0, tile(0))
                        norm.root_at_once(dv, 0)
                        norm.normalise(dv, 0, [(xn[0][:, :], whole)])
                    clear_r(T, not fresh)
                    factor(T, 0, not fresh)
                    keep_v(T)
                    for c in range(9):
                        if 1 <= c < LEVELS:
                            factor(T, c, not (fresh and c < 2))
                        place(T, c, 9 * p + c)
                        if not fresh and c == 1:
                            residual(T - 1, 1 - p)
                        if not fresh and c == 3:
                            centre2(T - 1)
                        if not fresh and c == 5:
                            norm2.root_at_once(dv, T - 1)
                        if not fresh and c == 6:
                            finish(T - 1)
                        if more and c == 4:
                            norm.centre(dv, T + 1, tile(T + 1))
                        if more and c == 6:
                            norm.root_at_once(dv, T + 1)
                    if more:
                        norm.normalise(dv, T + 1, [(xn[1 - p][:, :], whole)])
                if last:
                    residual(T, 1)
                    centre2(T)
                    norm2.root_at_once(dv, T)
                    finish(T)

            super_steps(dv, NT // 2, body)


A1_SIGNALS = ["q_ready", "k_ready", "logit_ready", "g_ready", "v_ready", "q_kept", "k_kept", "v_kept", "g_kept",
              "log_step", "log_asked", "exp_done", "log_done", "gk_ready", "cum_ready", "cum_kept", "exponent_spread",
              "decay_ready", "exp_ready", "masked", "qk_ready", "pairs_ready", "pv_done", "o_kept", "ms_ready",
              "log_ms", "rms_ready", "scaled", "gated", "y_ready", "x_updated"]


def head_gla_pass(nc, x, ones, ident, banks, w, sg, NT, tag):
    BLK, H, DK, DV = TILE // P, 4, 32, 64
    PAIRS = 4
    WIDE = SEQ + P
    with ExitStack() as ctx:
        def sb(name, shape, dt=F32):
            return ctx.enter_context(nc.sbuf_tensor(f"{tag}_{name}", shape, dt))

        xn = [sb(f"xn{i}", [P, TILE]) for i in range(2)]
        norm = Norm(sb, ones, ident, banks[0], sg, TILE)
        q, k, v = sb("q", [P, TILE]), sb("k", [P, TILE]), sb("v", [P, BLK, H * DV])
        silu = [[sb(f"silu{p}{c}", [P, TILE]) for c in range(2)] for p in range(2)]
        lo, neg, low, e1, l1, lmin, gk = (sb(n, [P, BLK, H]) for n in ("lo", "neg", "low", "e1", "l1", "lmin", "gk"))
        cum = sb("cum", [P, BLK, H])
        dec = [sb(f"dec{i}", [P, 2, WIDE]) for i in range(2)]
        pairs = [sb(f"pairs{i}", [P, WIDE]) for i in range(2)]
        o = [sb(f"o{c}", [P, TILE]) for c in range(2)]
        osq = [sb(f"osq{c}", [P, TILE]) for c in range(2)]
        lms, rms = sb("lms", [P, TILE]), [sb(f"rms{c}", [P, TILE]) for c in range(2)]
        t1, t2 = [sb(f"t1{c}", [P, TILE]) for c in range(2)], [sb(f"t2{c}", [P, TILE]) for c in range(2)]
        logit_ps = banks[0][:, 0:BLK * H].rearrange("p (b h) -> p b h", b=BLK)
        cum_ps = banks[0][:, 64:64 + BLK * H].rearrange("p (b h) -> p b h", b=BLK)
        block = ctx.enter_context(nc.Block())

        def tile(t):
            return x[:, bass.ds(t * TILE, TILE)]

        @block.tensor
        def _(pe):
            def project(T, p, before):
                pe.wait_ge(sg["xn_ready"], T + 1)
                for b in range(BLK):
                    mm = pe.matmul(logit_ps[:, b, :], xn[p][:, b * P:(b + 1) * P], w["wgk"][:, :],
                                   start=True, stop=True)
                mm.then_inc(sg["logit_ready"], 1)
                pe.matmul(banks[1][:, :], w["wq"][:, :], xn[p][:, :], start=True, stop=True).then_inc(sg["q_ready"], 1)
                pe.matmul(banks[2][:, :], w["wk"][:, :], xn[p][:, :], start=True, stop=True).then_inc(sg["k_ready"], 1)
                for c in range(2):
                    pe.matmul(banks[3 + c][:, :], w["wg"][:, c, :], xn[p][:, :], start=True, stop=True)\
                        .then_inc(sg["g_ready"], 1)
                if before:
                    pe.wait_ge(sg["o_kept"], 2 * T)
                for b in range(BLK):
                    pe.matmul(banks[5 + b // 2][:, (b % 2) * 256:(b % 2 + 1) * 256], xn[p][:, b * P:(b + 1) * P],
                              w["wv"][:, :], start=True, stop=True).then_inc(sg["v_ready"], 1)

            def running_sum(T):
                pe.wait_ge(sg["gk_ready"], T + 1)
                for b in range(BLK):
                    if b % 2:
                        pe.matmul(cum_ps[:, b, :], w["tri"][:, P:2 * P], gk[:, b - 1, :], start=True, stop=False)
                    mm = pe.matmul(cum_ps[:, b, :], w["tri"][:, 0:P], gk[:, b, :], start=(b % 2 == 0), stop=True)
                mm.then_inc(sg["cum_ready"], 1)

            def spread(T, j):
                if j < 2:
                    pe.wait_ge(sg["q_kept"], T + 1)
                    pe.wait_ge(sg["k_kept"], T + 1)
                else:
                    pe.wait_ge(sg["decay_ready"], T * PAIRS + j - 1)
                for c in range(2):
                    b, h = j // 2, 2 * (j % 2) + c
                    out = banks[1 + j % 2][:, c * SEQ:(c + 1) * SEQ]
                    pe.matmul(out, gk[:, 2 * b, h:h + 1].broadcast_to((P, P)), w["tri"][:, :],
                              start=True, stop=False)
                    mm = pe.matmul(out[:, P:SEQ], gk[:, 2 * b + 1, h:h + 1].broadcast_to((P, P)),
                                   w["tri"][:, 0:P], start=False, stop=True)
                mm.then_inc(sg["exponent_spread"], 1)

            def scores(T, j, c):
                b, h, n = j // 2, 2 * (j % 2) + c, 2 * j + c
                rows = slice(DK * h, DK * h + DK)
                if n < 2:
                    pe.wait_ge(sg["g_kept"], 2 * T + n + 1)
                else:
                    pe.wait_ge(sg["pairs_ready"], T * 8 + n - 1)
                at = b * SEQ
                out = banks[3 + n % 2]
                pe.matmul(out[:, 0:SEQ], k[rows, at:at + P], q[rows, at:at + SEQ], start=True, stop=True)
                pe.matmul(out[:, SEQ:WIDE], k[rows, at + P:at + SEQ], q[rows, at + P:at + SEQ],
                          start=True, stop=True).then_inc(sg["qk_ready"], 1)

            def values(T, j, c):
                b, h, n = j // 2, 2 * (j % 2) + c, 2 * j + c
                pe.wait_ge(sg["pairs_ready"], T * 8 + n + 1)
                if n == 0:
                    pe.wait_ge(sg["v_kept"], 2 * T + 2)
                out = banks[5 + j % 2][DV * c:DV * (c + 1), b * SEQ:(b + 1) * SEQ]
                cut = slice(DV * h, DV * (h + 1))
                pe.matmul(out, v[:, 2 * b, cut], pairs[n % 2][:, 0:SEQ], start=True, stop=False)
                pe.matmul(out[:, P:SEQ], v[:, 2 * b + 1, cut], pairs[n % 2][:, SEQ:WIDE], start=False, stop=True)\
                    .then_inc(sg["pv_done"], 1)

            def mean_square(T, c):
                pe.wait_ge(sg["o_kept"], 2 * T + c + 1)
                if c:
                    pe.wait_ge(sg["rms_ready"], 2 * T + 1)
                elif not (isinstance(T, int) and T == 0):
                    pe.wait_ge(sg["x_updated"], T)
                pe.matmul(banks[7][:, :], w["head_mean"][:, :], osq[c][:, :], start=True, stop=True)\
                    .then_inc(sg["ms_ready"], 1)

            def output(T):
                pe.wait_ge(sg["gated"], 2 * T + 2)
                pe.matmul(banks[7][:, :], w["wo"][:, 0, :], t2[0][:, :], start=True, stop=False)
                pe.matmul(banks[7][:, :], w["wo"][:, 1, :], t2[1][:, :], start=False, stop=True)\
                    .then_inc(sg["y_ready"], 1)

            def body(s, first, last):
                for p in range(2):
                    T = 2 * s + p
                    fresh, more = first and p == 0, not (last and p == 1)
                    if fresh:
                        norm.mean(pe, tile(0))
                        norm.var(pe, 0)
                        norm.spread(pe, 0)
                    project(T, p, not fresh)
                    if not fresh:
                        mean_square(T - 1, 0)
                    running_sum(T)
                    spread(T, 0)
                    spread(T, 1)
                    if not fresh:
                        mean_square(T - 1, 1)
                    for j in range(PAIRS):
                        scores(T, j, 0)
                        scores(T, j, 1)
                        if j + 2 < PAIRS:
                            spread(T, j + 2)
                        if j == 2 and more:
                            norm.var(pe, T + 1)
                        if j == 3 and more:
                            norm.spread(pe, T + 1)
                        values(T, j, 0)
                        values(T, j, 1)
                        if j == 0 and not fresh:
                            output(T - 1)
                        if j == 0 and more:
                            pe.wait_ge(sg["cum_kept"], T + 1)
                            norm.mean(pe, tile(T + 1))
                if last:
                    mean_square(T, 0)
                    mean_square(T, 1)
                    output(T)

            super_steps(pe, NT // 2, body)

        @block.scalar
        def _(ac):
            def keep_qk(T, before):
                if before:
                    ac.wait_ge(sg["qk_ready"], T * 8)
                ac.wait_ge(sg["q_ready"], T + 1)
                ac.activation(q[:, :], banks[1][:, :], ACT.Copy, scale=float(DK) ** -0.5).then_inc(sg["q_kept"], 1)
                ac.wait_ge(sg["k_ready"], T + 1)
                ac.activation(k[:, :], banks[2][:, :], ACT.Copy).then_inc(sg["k_kept"], 1)

            def log_gate(T):
                ac.wait_ge(sg["log_asked"], T + 1)
                ac.activation(e1[:, :, :], low[:, :, :], ACT.Exp).then_inc(sg["exp_done"], 1)
                ac.wait_ge(sg["exp_done"], T + 1)
                ac.activation(l1[:, :, :], e1[:, :, :], ACT.Ln, bias=1.0).then_inc(sg["log_done"], 1)

            def keep_g_v(T, p):
                for c in range(2):
                    ac.wait_ge(sg["g_ready"], 2 * T + c + 1)
                    ac.activation(silu[p][c][:, :], banks[3 + c][:, :], ACT.Silu).then_inc(sg["g_kept"], 1)
                for c in range(2):
                    ac.wait_ge(sg["v_ready"], 4 * T + 2 * c + 2)
                    ac.activation(v[:, 2 * c:2 * c + 2, :],
                                  banks[5 + c][:, :].rearrange("p (b e) -> p b e", b=2), ACT.Copy)\
                        .then_inc(sg["v_kept"], 1)

            def root_mean(T, c):
                ac.wait_ge(sg["ms_ready"], 2 * T + c + 1)
                ac.activation(lms[:, :], banks[7][:, :], ACT.Ln, bias=ones.eps[:, :]).then_inc(sg["log_ms"], 1)
                ac.wait_ge(sg["log_ms"], 2 * T + c + 1)
                ac.activation(rms[c][:, :], lms[:, :], ACT.Exp, scale=-0.5).then_inc(sg["rms_ready"], 1)

            def decay(T, j):
                ac.wait_ge(sg["decay_ready"], T * PAIRS + j + 1)
                ac.activation(dec[j % 2][:, :, :], dec[j % 2][:, :, :], ACT.Exp).then_inc(sg["exp_ready"], 1)

            def keep_o(T, before):
                if before:
                    ac.wait_ge(sg["gated"], 2 * T)
                for c in range(2):
                    ac.wait_ge(sg["pv_done"], T * 8 + 6 + 2 * c)
                    ac.activation(o[c][:, :], banks[5 + c][:, :], ACT.Copy)
                    ac.activation(osq[c][:, :], banks[5 + c][:, :], ACT.Square).then_inc(sg["o_kept"], 1)

            def body(s, first, last):
                for p in range(2):
                    T = 2 * s + p
                    fresh, more = first and p == 0, not (last and p == 1)
                    if fresh:
                        norm.square(ac, 0)
                    keep_qk(T, not fresh)
                    log_gate(T)
                    keep_g_v(T, p)
                    if not fresh:
                        root_mean(T - 1, 0)
                    decay(T, 0)
                    if not fresh:
                        root_mean(T - 1, 1)
                    decay(T, 1)
                    decay(T, 2)
                    if more:
                        norm.square(ac, T + 1)
                    decay(T, 3)
                    keep_o(T, not fresh)
                if last:
                    root_mean(T, 0)
                    root_mean(T, 1)

            super_steps(ac, NT // 2, body)

        @block.gpsimd
        def _(pool):
            def mask(T, j):
                pool.wait_ge(sg["exp_ready"], T * PAIRS + j + 1)
                for at in (0, SEQ):
                    cut = dec[j % 2][:, :, at:at + P]
                    ins = pool.tensor_tensor(cut, cut, w["tri2"][:, :, :], ALU.mult)
                ins.then_inc(sg["masked"], 1)

            def body(s, first, last):
                for p in range(2):
                    for j in range(PAIRS):
                        mask(2 * s + p, j)

            super_steps(pool, NT // 2, body)

        @block.vector
        def _(dv):
            def chain(ins, T, k):
                ins.then_inc(sg["log_step"], 1)
                dv.wait_ge(sg["log_step"], T * 3 + k + 1)

            def log_gate_in(T):
                dv.wait_ge(sg["logit_ready"], T + 1)
                chain(dv.tensor_tensor(lo[:, :, :], logit_ps, w["bgk"][:, :, :], ALU.add), T, 0)
                chain(dv.tensor_scalar(neg[:, :, :], lo[:, :, :], -1.0, None, ALU.mult), T, 1)
                dv.tensor_scalar(lmin[:, :, :], lo[:, :, :], 0.0, None, ALU.min)
                dv.tensor_tensor(low[:, :, :], lo[:, :, :], neg[:, :, :], ALU.min).then_inc(sg["log_asked"], 1)

            def log_gate_out(T):
                dv.wait_ge(sg["log_done"], T + 1)
                chain(dv.tensor_tensor(lo[:, :, :], lmin[:, :, :], l1[:, :, :], ALU.subtract), T, 2)
                dv.tensor_scalar(gk[:, :, :], lo[:, :, :], 1.0 / 16.0, None, ALU.mult).then_inc(sg["gk_ready"], 1)

            def keep_sum(T):
                dv.wait_ge(sg["cum_ready"], T + 1)
                dv.tensor_copy(cum[:, :, :], cum_ps).then_inc(sg["cum_kept"], 1)
                dv.wait_ge(sg["cum_kept"], T + 1)

            def exponent(T, j, before):
                dv.wait_ge(sg["exponent_spread"], T * PAIRS + j + 1)
                if before:
                    dv.wait_ge(sg["pairs_ready"], T * 8 + 2 * j - 2)
                for c in range(2):
                    b, h = j // 2, 2 * (j % 2) + c
                    src = banks[1 + j % 2][:, c * SEQ:(c + 1) * SEQ]
                    dv.tensor_scalar(dec[j % 2][:, c, 0:SEQ], src, cum[:, 2 * b, h:h + 1], 0.0,
                                     ALU.subtract, ALU.min)
                    ins = dv.tensor_scalar(dec[j % 2][:, c, SEQ:WIDE], src[:, P:SEQ], cum[:, 2 * b + 1, h:h + 1],
                                           0.0, ALU.subtract, ALU.min)
                ins.then_inc(sg["decay_ready"], 1)

            def weigh(T, j, c, before):
                n = 2 * j + c
                dv.wait_ge(sg["qk_ready"], T * 8 + n + 1)
                dv.wait_ge(sg["masked"], T * PAIRS + j + 1)
                if before:
                    dv.wait_ge(sg["pv_done"], T * 8 + n - 1)
                dv.tensor_tensor(pairs[n % 2][:, :], dec[j % 2][:, c, :], banks[3 + n % 2][:, 0:WIDE], ALU.mult)\
                    .then_inc(sg["pairs_ready"], 1)

            def gate(T, c, p):
                dv.wait_ge(sg["rms_ready"], 2 * T + c + 1)
                dv.scalar_tensor_tensor(out=t1[c][:, :], in0=o[c][:, :], scalar=w["gnorm"][:, 0:1], in1=rms[c][:, :],
                                        op0=ALU.mult, op1=ALU.mult).then_inc(sg["scaled"], 1)
                dv.wait_ge(sg["scaled"], 2 * T + c + 1)
                dv.tensor_tensor(t2[c][:, :], t1[c][:, :], silu[p][c][:, :], ALU.mult).then_inc(sg["gated"], 1)

            def update(T):
                dv.wait_ge(sg["y_ready"], T + 1)
                dv.tensor_tensor(tile(T), tile(T), banks[7][:, :], ALU.add).then_inc(sg["x_updated"], 1)

            def body(s, first, last):
                for p in range(2):
                    T = 2 * s + p
                    fresh, more = first and p == 0, not (last and p == 1)
                    if fresh:
                        norm.centre(dv, 0, tile(0))
                        norm.root_at_once(dv, 0)
                        norm.normalise(dv, 0, [(xn[0][:, :], whole)])
                    log_gate_in(T)
                    log_gate_out(T)
                    keep_sum(T)
                    exponent(T, 0, not fresh)
                    if not fresh:
                        gate(T - 1, 0, 1 - p)
                    exponent(T, 1, not fresh)
                    weigh(T, 0, 0, not fresh)
                    weigh(T, 0, 1, not fresh)
                    if not fresh:
                        gate(T - 1, 1, 1 - p)
                    for j in range(1, PAIRS):
                        if j + 1 < PAIRS:
                            exponent(T, j + 1, True)
                        weigh(T, j, 0, True)
                        weigh(T, j, 1, True)
                        if j == 1 and not fresh:
                            update(T - 1)
                        if j == 1 and more:
                            norm.centre(dv, T + 1, tile(T + 1))
                        if j == 2 and more:
                            norm.root_at_once(dv, T + 1)
                    if more:
                        norm.normalise(dv, T + 1, [(xn[1 - p][:, :], whole)])
                if last:
                    gate(T, 0, 1)
                    gate(T, 1, 1)
                    update(T)

            super_steps(dv, NT // 2, body)


A2_SIGNALS = ["q_ready", "k_ready", "v_ready", "q_kept", "k_kept", "v_kept", "keys_ready", "scores_ready", "maxed",
              "shifted", "exp_ready", "summed", "inverted2", "normed", "turned", "turned_kept", "values_ready",
              "pv_done", "o_kept", "y_ready", "y_kept", "x_updated"]


def window_attention_pass(nc, x, ones, ident, banks, w, twice_bo, sg, NT, tag):
    WIN, SHIFT, H = 64, 32, 8
    PAIRS, WINDOWS = TILE // (2 * WIN), TILE // WIN
    KEPT = SEQ - SHIFT
    with ExitStack() as ctx:
        def sb(name, shape, dt=F32):
            return ctx.enter_context(nc.sbuf_tensor(f"{tag}_{name}", shape, dt))

        xs = [sb(f"xs{i}", [P, TILE]) for i in range(2)]
        norm = WideNorm(sb, ones, banks[0], sg, TILE)
        q, k, vd = sb("q", [P, TILE]), sb("k", [P, TILE]), sb("vd", [P, WINDOWS, P])
        keys = [sb(f"keys{i}", [P, H, WIN]) for i in range(4)]
        vals = [sb(f"vals{i}", [P, H // 2, P]) for i in range(4)]
        prob = [sb(f"prob{i}", [P, H, WIN]) for i in range(2)]
        top, total, inv = ([sb(f"{n}{i}", [P, H, 1]) for i in range(2)] for n in ("top", "total", "invt"))
        turned = [sb(f"turned{i}", [P, H // 2, P]) for i in range(2)]
        o, y = sb("o", [P, TILE]), sb("y", [P, TILE])
        block = ctx.enter_context(nc.Block())

        def tile(t):
            return x[:, bass.ds(t * TILE, TILE)].rearrange("p (b n) -> p b n", n=SEQ)

        def by_seq(tensor):
            return tensor[:, :].rearrange("p (b n) -> p b n", n=SEQ)

        def rolled(out):
            return [(by_seq(out)[:, :, 0:KEPT], lambda v: by_seq(v)[:, :, SHIFT:SEQ]),
                    (by_seq(out)[:, :, KEPT:SEQ], lambda v: by_seq(v)[:, :, 0:SHIFT])]

        @block.tensor
        def _(pe):
            def project(T, p, before):
                pe.wait_ge(sg["xn_ready"], T + 1)
                pe.matmul(banks[1][:, :], w["wq"][:, :], xs[p][:, :], start=True, stop=True).then_inc(sg["q_ready"], 1)
                if before:
                    pe.wait_ge(sg["y_kept"], T - 1)
                pe.matmul(banks[2][:, :], w["wk"][:, :], xs[p][:, :], start=True, stop=True).then_inc(sg["k_ready"], 1)
                if before:
                    pe.wait_ge(sg["turned_kept"], T * PAIRS)
                for n in range(WINDOWS):
                    for c in range(2):
                        mm = pe.matmul(banks[3 + n // 4][c * WIN:(c + 1) * WIN, (n % 4) * P:(n % 4 + 1) * P],
                                       xs[p][:, n * WIN:(n + 1) * WIN], w["wv"][:, :], start=True, stop=True)
                    if n % 4 == 3:
                        mm.then_inc(sg["v_ready"], 1)

            def scores(T, j, before):
                if j == 0:
                    pe.wait_ge(sg["q_kept"], T + 1)
                if before:
                    pe.wait_ge(sg["shifted"], T * PAIRS + j - 1)
                for c in range(2):
                    n = 2 * j + c
                    pe.wait_ge(sg["keys_ready"], T * WINDOWS + n + 1)
                    mm = pe.matmul(banks[5 + j % 2][c * WIN:(c + 1) * WIN, :], q[:, n * WIN:(n + 1) * WIN],
                                   keys[n % 4][:, :, :].rearrange("p h n -> p (h n)"), start=True, stop=True)
                mm.then_inc(sg["scores_ready"], 1)

            def turn(T, j):
                pe.wait_ge(sg["normed"], T * PAIRS + j + 1)
                if j < 2:
                    pe.wait_ge(sg["v_kept"], 2 * T + 2)
                else:
                    pe.wait_ge(sg["turned_kept"], T * PAIRS + j - 1)
                for c in range(H // 2):
                    mm = pe.transpose(banks[3 + j % 2][:, c * P:(c + 1) * P],
                                      prob[j % 2][:, 2 * c:2 * c + 2, :].rearrange("p h n -> p (h n)"), ident[:, :])
                mm.then_inc(sg["turned"], 1)

            def values(T, j):
                pe.wait_ge(sg["turned_kept"], T * PAIRS + j + 1)
                if j == 0 and not (isinstance(T, int) and T == 0):
                    pe.wait_ge(sg["o_kept"], T)
                for c in range(2):
                    n = 2 * j + c
                    pe.wait_ge(sg["values_ready"], T * WINDOWS + n + 1)
                    for h in range(H // 2):
                        mm = pe.matmul(banks[7][:, n * WIN:(n + 1) * WIN], vals[n % 4][:, h, :],
                                       turned[j % 2][:, h, c * WIN:(c + 1) * WIN], start=(h == 0),
                                       stop=(h == H // 2 - 1))
                mm.then_inc(sg["pv_done"], 1)

            def output(T):
                pe.wait_ge(sg["o_kept"], T + 1)
                pe.matmul(banks[2][:, :], w["wo"][:, :], o[:, :], start=True, stop=True).then_inc(sg["y_ready"], 1)

            def body(s, first, last):
                for p in range(2):
                    T = 2 * s + p
                    fresh, more = first and p == 0, not (last and p == 1)
                    if fresh:
                        norm.mean(pe, x[:, 0:TILE])
                        norm.var(pe, 0)
                    project(T, p, not fresh)
                    scores(T, 0, not fresh)
                    scores(T, 1, not fresh)
                    if not fresh:
                        output(T - 1)
                    for j in range(PAIRS):
                        turn(T, j)
                        if j + 2 < PAIRS:
                            scores(T, j + 2, True)
                        if j == 0 and more:
                            norm.mean(pe, x[:, bass.ds((T + 1) * TILE, TILE)])
                        if j == 2 and more:
                            norm.var(pe, T + 1)
                        values(T, j)
                if last:
                    output(T)

            super_steps(pe, NT // 2, body)

        @block.scalar
        def _(ac):
            def keep_qk(T):
                ac.wait_ge(sg["q_ready"], T + 1)
                ac.activation(q[:, :], banks[1][:, :], ACT.Identity, bias=w["bq"][:, 0:1]).then_inc(sg["q_kept"], 1)
                ac.wait_ge(sg["k_ready"], T + 1)
                ac.activation(k[:, :], banks[2][:, :], ACT.Identity, bias=w["bk"][:, 0:1]).then_inc(sg["k_kept"], 1)

            def exps(T, j):
                ac.wait_ge(sg["shifted"], T * PAIRS + j + 1)
                ac.activation(prob[j % 2][:, :, :], prob[j % 2][:, :, :], ACT.Exp, scale=0.25)\
                    .then_inc(sg["exp_ready"], 1)

            def keep_turned(T, j, before):
                ac.wait_ge(sg["turned"], T * PAIRS + j + 1)
                if before:
                    ac.wait_ge(sg["pv_done"], T * PAIRS + j - 1)
                ac.activation(turned[j % 2][:, :, :], banks[3 + j % 2][:, :].rearrange("p (h n) -> p h n", n=P),
                              ACT.Copy).then_inc(sg["turned_kept"], 1)

            def keep_o(T):
                ac.wait_ge(sg["pv_done"], (T + 1) * PAIRS)
                ac.activation(o[:, :], banks[7][:, :], ACT.Copy).then_inc(sg["o_kept"], 1)

            def keep_y(T):
                ac.wait_ge(sg["y_ready"], T + 1)
                if not (isinstance(T, int) and T == 0):
                    ac.wait_ge(sg["x_updated"], T)
                ac.activation(y[:, :], banks[2][:, :], ACT.Identity, scale=2.0, bias=twice_bo[:, 0:1])\
                    .then_inc(sg["y_kept"], 1)

            def body(s, first, last):
                for p in range(2):
                    T = 2 * s + p
                    fresh, more = first and p == 0, not (last and p == 1)
                    if fresh:
                        norm.square(ac, 0)
                        norm.root(ac, 0)
                    keep_qk(T)
                    exps(T, 0)
                    if not fresh:
                        keep_y(T - 1)
                    for j in range(PAIRS):
                        if j + 1 < PAIRS:
                            exps(T, j + 1)
                        if j == 1 and more:
                            norm.square(ac, T + 1)
                        if j == 3 and more:
                            norm.root(ac, T + 1)
                        keep_turned(T, j, not (fresh and j < 2))
                    keep_o(T)
                if last:
                    keep_y(T)

            super_steps(ac, NT // 2, body)

        @block.gpsimd
        def _(pool):
            def lay_keys(T, n, before):
                if n == 0:
                    pool.wait_ge(sg["k_kept"], T + 1)
                if before and n % 2 == 0:
                    pool.wait_ge(sg["scores_ready"], T * PAIRS + n // 2 - 1)
                one = k[:, n * WIN:(n + 1) * WIN].unsqueeze(1).broadcast_to((P, H, WIN))
                pool.tensor_tensor(keys[n % 4][:, :, :], one, w["head_keys"][:, :, :], ALU.mult)\
                    .then_inc(sg["keys_ready"], 1)

            def body(s, first, last):
                for p in range(2):
                    for n in range(WINDOWS):
                        lay_keys(2 * s + p, n, not (first and p == 0 and n < 4))

            super_steps(pool, NT // 2, body)

        @block.vector
        def _(dv):
            def keep_v(T):
                for c in range(2):
                    dv.wait_ge(sg["v_ready"], 2 * T + c + 1)
                    dv.tensor_tensor(vd[:, 4 * c:4 * c + 4, :], banks[3 + c][:, :].rearrange("p (n d) -> p n d", d=P),
                                     w["bv"][:, :, :], ALU.add).then_inc(sg["v_kept"], 1)

            def shift(T, j, before):
                src = banks[5 + j % 2][:, :].rearrange("p (h n) -> p h n", n=WIN)
                dv.wait_ge(sg["scores_ready"], T * PAIRS + j + 1)
                dv.tensor_reduce(top[j % 2][:, :, :], src, AX_X, ALU.max).then_inc(sg["maxed"], 1)
                dv.wait_ge(sg["maxed"], T * PAIRS + j + 1)
                if before:
                    dv.wait_ge(sg["turned"], T * PAIRS + j - 1)
                dv.tensor_tensor(prob[j % 2][:, :, :], src, top[j % 2][:, :, :].broadcast_to((P, H, WIN)),
                                 ALU.subtract).then_inc(sg["shifted"], 1)

            def lay_values(T, n, before):
                if before:
                    dv.wait_ge(sg["pv_done"], T * PAIRS + n // 2 - 1)
                if n == 0:
                    dv.wait_ge(sg["v_kept"], 2 * T + 2)
                one = vd[:, n, :].unsqueeze(1).broadcast_to((P, H // 2, P))
                dv.tensor_tensor(vals[n % 4][:, :, :], one, w["head_vals"][:, :, :], ALU.mult)\
                    .then_inc(sg["values_ready"], 1)

            def normalise(T, j):
                dv.wait_ge(sg["exp_ready"], T * PAIRS + j + 1)
                dv.tensor_reduce(total[j % 2][:, :, :], prob[j % 2][:, :, :], AX_X, ALU.add).then_inc(sg["summed"], 1)
                dv.wait_ge(sg["summed"], T * PAIRS + j + 1)
                dv.reciprocal(inv[j % 2][:, :, :], total[j % 2][:, :, :]).then_inc(sg["inverted2"], 1)
                dv.wait_ge(sg["inverted2"], T * PAIRS + j + 1)
                dv.tensor_tensor(prob[j % 2][:, :, :], prob[j % 2][:, :, :],
                                 inv[j % 2][:, :, :].broadcast_to((P, H, WIN)), ALU.mult).then_inc(sg["normed"], 1)

            def update(T):
                dv.wait_ge(sg["y_kept"], T + 1)
                kept, wrapped = tile(T)[:, :, SHIFT:SEQ], tile(T)[:, :, 0:SHIFT]
                dv.tensor_tensor(kept, kept, by_seq(y)[:, :, 0:KEPT], ALU.add)
                dv.tensor_tensor(wrapped, wrapped, by_seq(y)[:, :, KEPT:SEQ], ALU.add).then_inc(sg["x_updated"], 1)

            def body(s, first, last):
                for p in range(2):
                    T = 2 * s + p
                    fresh, more = first and p == 0, not (last and p == 1)
                    if fresh:
                        norm.centre(dv, 0, x[:, 0:TILE])
                        norm.normalise(dv, 0, rolled(xs[0]))
                    keep_v(T)
                    shift(T, 0, not fresh)
                    for j in range(PAIRS):
                        if j + 1 < PAIRS:
                            shift(T, j + 1, not (fresh and j == 0))
                        for n in (2 * j, 2 * j + 1):
                            lay_values(T, n, not (fresh and j < 2))
                        normalise(T, j)
                        if j == 0 and not fresh:
                            update(T - 1)
                        if j == 1 and more:
                            norm.centre(dv, T + 1, x[:, bass.ds((T + 1) * TILE, TILE)])
                    if more:
                        norm.normalise(dv, T + 1, rolled(xs[1 - p]))
                if last:
                    update(T)

            super_steps(dv, NT // 2, body)


A0_SIGNALS = ["r_in", "hn_in", "z_in", "s_in", "r_out", "z_out", "sg_out", "rh_done", "n_in", "n_out", "keep_done",
              "carry_done", "fresh_done", "h_ready", "s_ready", "projected", "in_ready", "in_kept", "gate_ready",
              "gate_kept", "y_ready", "y_taken", "summed", "x_updated", "cleared"]
STEPS = 16


def recurrent_pass(nc, x, ones, ident, banks, w, wide, sg, B, tag):
    CH = SEQ // STEPS
    N = STEPS * B
    S = w["a"].shape[0]
    with ExitStack() as ctx:
        def sb(name, shape, dt=F32):
            return ctx.enter_context(nc.sbuf_tensor(f"{tag}_{name}", shape, dt))

        xn = [sb(f"xn{i}", [P, N]) for i in range(2)]
        norm = Norm(sb, ones, ident, banks[7], sg, N)
        i_n = [sb(f"in{i}", [P, N]) for i in range(2)]
        hist = [sb(f"hist{i}", [P, STEPS, B]) for i in range(2)]
        shist = [sb(f"shist{i}", [S, STEPS, B]) for i in range(2)]
        r, z, n_, rh, npre, keep, carry, fresh_ = ([sb(f"{n}{i}", [P, B]) for i in range(2)] for n in
                                                   ("r", "z", "n", "rh", "npre", "keep", "carry", "fresh"))
        sgm = [sb(f"sgm{i}", [S, B]) for i in range(2)]
        gates = [sb(f"gate{i}", [P, N]) for i in range(2)]
        fa, fb, fs = sb("fa", [P, N]), sb("fb", [P, N]), sb("fs", [P, N])
        block = ctx.enter_context(nc.Block())
        by_seq = x[:, :].rearrange("p (b n) -> p b n", n=SEQ)

        def chunk(c):
            return by_seq[:, :, bass.ds(c * STEPS, STEPS)]

        def bst(tensor):
            return tensor[:, 0:N].rearrange("p (b t) -> p b t", t=STEPS)

        def tsb(tensor):
            return tensor[:, 0:N].rearrange("p (t b) -> p b t", t=STEPS)

        def before_step(p, t, tensors):
            return tensors[p][:, t - 1, :] if t else tensors[1 - p][:, STEPS - 1, :]

        @block.tensor
        def _(pe):
            def project(c, p):
                pe.wait_ge(sg["xn_ready"], c + 1)
                pe.matmul(banks[p][:, 0:N], w["w_ih"][:, 0, :], xn[p][:, :], start=True, stop=False,
                          skip_group_check=True)
                pe.matmul(banks[2 + p][:, 0:N], w["w_ih"][:, 1, :], xn[p][:, :], start=True, stop=False,
                          skip_group_check=True)
                pe.matmul(banks[4 + p][0:S, 0:N], w["bw"][:, :], xn[p][:, :], start=True, stop=False,
                          skip_group_check=True)
                pe.matmul(banks[7][:, 0:N], w["w_ih"][:, 2, :], xn[p][:, :], start=True, stop=True)\
                    .then_inc(sg["in_ready"], 1)

            def step(c, t, p):
                at = c * STEPS + t
                cols = slice(t * B, (t + 1) * B)
                h = before_step(p, t, hist)
                pe.wait_ge(sg["h_ready"], at + 1)
                pe.matmul(banks[p][:, cols], w["w_hh"][:, 0, :], h, start=False, stop=True,
                          skip_group_check=True).then_inc(sg["r_in"], 1)
                pe.matmul(banks[6][:, (t % 2) * B:(t % 2 + 1) * B], w["w_hh"][:, 2, :], h, start=True, stop=True)\
                    .then_inc(sg["hn_in"], 1)
                pe.matmul(banks[2 + p][:, cols], w["w_hh"][:, 1, :], h, start=False, stop=True,
                          skip_group_check=True).then_inc(sg["z_in"], 1)
                pe.wait_ge(sg["s_ready"], at + 1)
                pe.matmul(banks[4 + p][0:S, cols], w["a"][:, :], before_step(p, t, shist), start=False, stop=True,
                          skip_group_check=True).then_inc(sg["s_in"], 1)

            def gate(c, p, g):
                if g == 0:
                    pe.wait_ge(sg["in_kept"], c + 1)
                else:
                    pe.wait_ge(sg["gate_kept"], 2 * c + 1)
                pe.matmul(banks[7][:, 0:N], w["gate"][:, g, :], xn[p][:, :], start=True, stop=True)\
                    .then_inc(sg["gate_ready"], 1)

            def outputs(c, p, kind):
                if kind == 0:
                    pe.wait_ge(sg["gate_kept"], 2 * c + 2)
                    pe.wait_ge(sg["s_ready"], (c + 1) * STEPS + 1)
                    pe.wait_ge(sg["h_ready"], (c + 1) * STEPS + 1)
                    pe.matmul(banks[7][:, 0:N], w["cw"][:, :], shist[p][:, :, :].rearrange("p t b -> p (t b)"),
                              start=True, stop=False)
                    pe.matmul(banks[7][:, 0:N], w["dw"][:, :], xn[p][:, :], start=False, stop=True)\
                        .then_inc(sg["y_ready"], 1)
                else:
                    pe.wait_ge(sg["y_taken"], 2 * c + 1)
                    pe.matmul(banks[7][:, 0:N], w["proj"][:, :], hist[p][:, :, :].rearrange("p t b -> p (t b)"),
                              start=True, stop=True).then_inc(sg["y_ready"], 1)

            def body(s, first, last):
                for p in range(2):
                    c = 2 * s + p
                    fresh, more = first and p == 0, not (last and p == 1)
                    if fresh:
                        norm.mean(pe, chunk(0))
                        norm.var(pe, 0)
                        norm.spread(pe, 0)
                        project(0, 0)
                    for t in range(STEPS):
                        step(c, t, p)
                        if not fresh and t in (1, 2):
                            if t == 1:
                                pe.wait_ge(sg["in_kept"], c + 1)
                            gate(c - 1, 1 - p, t - 1)
                        if not fresh and t in (3, 4):
                            outputs(c - 1, 1 - p, t - 3)
                        if more and t == 6:
                            if fresh:
                                pe.wait_ge(sg["in_kept"], 1)
                            else:
                                pe.wait_ge(sg["y_taken"], 2 * c)
                            norm.mean(pe, chunk(c + 1))
                        if more and t == 8:
                            norm.var(pe, c + 1)
                        if more and t == 12:
                            norm.spread(pe, c + 1)
                        if more and t == 14:
                            project(c + 1, 1 - p)
                if last:
                    gate(c, 1, 0)
                    gate(c, 1, 1)
                    outputs(c, 1, 0)
                    outputs(c, 1, 1)

            super_steps(pe, CH // 2, body)

        @block.scalar
        def _(ac):
            def keep_in(c, p):
                ac.wait_ge(sg["in_ready"], c + 1)
                ac.activation(i_n[p][:, :], banks[7][:, 0:N], ACT.Identity, bias=w["b_in"][:, 0:1])\
                    .then_inc(sg["in_kept"], 1)

            def step(c, t, p):
                at = c * STEPS + t
                cols = slice(t * B, (t + 1) * B)
                ac.wait_ge(sg["r_in"], at + 1)
                ac.activation(r[t % 2][:, :], banks[p][:, cols], ACT.Sigmoid, bias=wide["b_r"][:, 0:1])\
                    .then_inc(sg["r_out"], 1)
                ac.wait_ge(sg["z_in"], at + 1)
                ac.activation(z[t % 2][:, :], banks[2 + p][:, cols], ACT.Sigmoid, bias=wide["b_z"][:, 0:1])\
                    .then_inc(sg["z_out"], 1)
                ac.wait_ge(sg["n_in"], at + 1)
                ac.activation(n_[t % 2][:, :], npre[t % 2][:, :], ACT.Tanh).then_inc(sg["n_out"], 1)
                ac.wait_ge(sg["s_in"], at + 1)
                ac.activation(sgm[t % 2][:, :], banks[4 + p][0:S, cols], ACT.Sigmoid, bias=w["bb"][:, 0:1])\
                    .then_inc(sg["sg_out"], 1)

            def keep_gate(c, g):
                ac.wait_ge(sg["gate_ready"], 2 * c + g + 1)
                if g == 0 and not (isinstance(c, int) and c == 0):
                    ac.wait_ge(sg["y_taken"], 2 * c)
                ac.activation(gates[g][:, :], banks[7][:, 0:N], ACT.Sigmoid, bias=w["gate_b"][:, g:g + 1])\
                    .then_inc(sg["gate_kept"], 1)

            def body(s, first, last):
                for p in range(2):
                    c = 2 * s + p
                    fresh, more = first and p == 0, not (last and p == 1)
                    if fresh:
                        norm.square(ac, 0)
                        keep_in(0, 0)
                    for t in range(STEPS):
                        step(c, t, p)
                        if not fresh and t in (1, 2):
                            keep_gate(c - 1, t - 1)
                        if more and t == 6:
                            norm.square(ac, c + 1)
                        if more and t == 14:
                            keep_in(c + 1, 1 - p)
                if last:
                    keep_gate(c, 0)
                    keep_gate(c, 1)

            super_steps(ac, CH // 2, body)

        @block.gpsimd
        def _(pool):
            def step(c, t, p):
                at = c * STEPS + t
                pool.wait_ge(sg["z_out"], at + 1)
                pool.tensor_tensor(keep[t % 2][:, :], z[t % 2][:, :], before_step(p, t, hist), ALU.mult)\
                    .then_inc(sg["keep_done"], 1)
                pool.tensor_scalar(carry[t % 2][:, :], z[t % 2][:, :], -1.0, 1.0, ALU.mult, ALU.add)\
                    .then_inc(sg["carry_done"], 1)

            def total(c):
                pool.wait_ge(sg["y_taken"], 2 * c + 2)
                pool.tensor_tensor(fs[:, :], fa[:, :], fb[:, :], ALU.add).then_inc(sg["summed"], 1)
                pool.wait_ge(sg["summed"], c + 1)
                pool.tensor_tensor(chunk(c), chunk(c), tsb(fs), ALU.add).then_inc(sg["x_updated"], 1)

            def body(s, first, last):
                for p in range(2):
                    c = 2 * s + p
                    fresh = first and p == 0
                    for t in range(STEPS):
                        step(c, t, p)
                        if not fresh and t == 6:
                            total(c - 1)
                if last:
                    total(c)

            super_steps(pool, CH // 2, body)

        @block.vector
        def _(dv):
            dv.memset(shist[1][:, STEPS - 1, :], 0.0).then_inc(sg["s_ready"], 1)
            dv.memset(hist[1][:, STEPS - 1, :], 0.0).then_inc(sg["h_ready"], 1)

            def step(c, t, p):
                at = c * STEPS + t
                cols = slice(t * B, (t + 1) * B)
                dv.wait_ge(sg["r_out"], at + 1)
                dv.wait_ge(sg["hn_in"], at + 1)
                dv.scalar_tensor_tensor(out=rh[t % 2][:, :], in0=banks[6][:, (t % 2) * B:(t % 2 + 1) * B],
                                        scalar=w["b_hn"][:, 0:1], in1=r[t % 2][:, :], op0=ALU.add, op1=ALU.mult)\
                    .then_inc(sg["rh_done"], 1)
                dv.wait_ge(sg["rh_done"], at + 1)
                if t == 0:
                    dv.wait_ge(sg["in_kept"], c + 1)
                dv.tensor_tensor(npre[t % 2][:, :], rh[t % 2][:, :], i_n[p][:, cols], ALU.add).then_inc(sg["n_in"], 1)
                dv.wait_ge(sg["n_out"], at + 1)
                dv.wait_ge(sg["carry_done"], at + 1)
                dv.tensor_tensor(fresh_[t % 2][:, :], carry[t % 2][:, :], n_[t % 2][:, :], ALU.mult)\
                    .then_inc(sg["fresh_done"], 1)
                dv.wait_ge(sg["fresh_done"], at + 1)
                dv.tensor_tensor(hist[p][:, t, :], fresh_[t % 2][:, :], keep[t % 2][:, :], ALU.add)\
                    .then_inc(sg["h_ready"], 1)
                dv.wait_ge(sg["sg_out"], at + 1)
                dv.scalar_tensor_tensor(out=shist[p][:, t, :], in0=banks[4 + p][0:S, cols],
                                        scalar=w["bb"][:, 0:1], in1=sgm[t % 2][:, :], op0=ALU.add, op1=ALU.mult)\
                    .then_inc(sg["s_ready"], 1)

            def take(c, kind):
                dv.wait_ge(sg["y_ready"], 2 * c + kind + 1)
                if kind == 0 and not (isinstance(c, int) and c == 0):
                    dv.wait_ge(sg["summed"], c)
                out, bias = ((fa, wide["b_ssm"]), (fb, w["proj_b"]))[kind]
                dv.scalar_tensor_tensor(out=out[:, :], in0=banks[7][:, 0:N], scalar=bias[:, 0:1],
                                        in1=gates[kind][:, :], op0=ALU.add, op1=ALU.mult).then_inc(sg["y_taken"], 1)

            def body(s, first, last):
                for p in range(2):
                    c = 2 * s + p
                    fresh, more = first and p == 0, not (last and p == 1)
                    if fresh:
                        norm.centre_view(dv, 0, chunk(0), bst)
                        norm.root_at_once(dv, 0)
                        norm.normalise(dv, 0, [(tsb(xn[0]), bst)])
                    for t in range(STEPS):
                        step(c, t, p)
                        if not fresh and t in (3, 4):
                            take(c - 1, t - 3)
                        if more and t == 6:
                            norm.centre_view(dv, c + 1, chunk(c + 1), bst)
                        if more and t == 9:
                            root = norm.root(dv, c + 1)
                        if more and t in (9, 10, 11):
                            for _ in range(4):
                                next(root, None)
                        if more and t == 12:
                            norm.normalise(dv, c + 1, [(tsb(xn[1 - p]), bst)])
                if last:
                    take(c, 0)
                    take(c, 1)

            super_steps(dv, CH // 2, body)


@contextmanager
def Signals(nc, tag, names):
    with ExitStack() as ctx:
        sems = {name: ctx.enter_context(nc.semaphore(f"{tag}_{name}")) for name in names}
        yield sems
        with nc.Block() as block:
            @block.gpsimd
            def _(pool):
                for sem in sems.values():
                    pool.sem_clear(sem)


class Ones:

    def __init__(self, tensor, eps):
        self.tensor, self.eps = tensor, eps

    def __getitem__(self, at):
        return self.tensor[at]


def constants():
    c = {}
    c["c_ones"] = np.full((P, P), 1.0 / P, np.float32)
    c["c_ident"] = np.eye(P, dtype=np.float32)
    for name, e, pair in (("sel8", 8, False), ("sel16", 16, True)):
        sel = np.zeros((3 * e, 8, P), np.float32)
        for g in range(8):
            for part in range(3):
                for p in range(P):
                    sel[part * e + (2 * g + p // 64 if pair else g), g, p] = 1.0
        c["c_" + name] = sel
    for e in (8, 16):
        c[f"c_rev{e}"] = np.broadcast_to(np.arange(e, 0, -1, dtype=np.float32), (P, 4, e)).copy()
    j, i = np.arange(P)[:, None], np.arange(TILE)[None, :] % P
    c["a3_mask_diag"] = (j == i).astype(np.int32)
    tri = (np.arange(P)[:, None] <= np.arange(P)[None, :]).astype(np.float32)
    c["a1_tri"] = np.concatenate([tri, np.ones((P, P), np.float32)], 1)
    c["a1_tri2"] = np.ascontiguousarray(np.broadcast_to(tri[:, None, :], (P, 2, P)))
    c["a1_head_mean"] = (j // 64 == np.arange(P)[None, :] // 64).astype(np.float32) / 64
    c["a2_head_keys"] = np.ascontiguousarray(
        np.broadcast_to((j // 16 == np.arange(8)[None, :])[:, :, None], (P, 8, 64)).astype(np.float32))
    head = 2 * np.arange(4)[None, :, None] + j[:, :, None] // 64
    c["a2_head_vals"] = (np.arange(P)[None, None, :] // 16 == head).astype(np.float32)
    masks = []
    for m in range(7):
        of_level = (j >> (m + 1) == i >> (m + 1)) & (j >> m & 1 == 0)
        masks.append(of_level[:, (np.arange(TILE) >> m) & 1 == 1])
    c["a3_mask"] = np.ascontiguousarray(np.stack(masks, 1).astype(np.int32))
    return c


def first_names(shapes):
    return [n for n in shapes if n in ("c_ones", "c_ident") or n[:3] == "f0_"]


def other_names(shapes):
    alone = ("x", "m1_w1", "m1_w2", "m2_wg", "m2_wu", "m2_wd", "m3_wg", "m3_wu", "m3_wd", "a3_mask_diag", "a3_mask")
    return [n for n in shapes if n not in alone and n not in first_names(shapes) and shapes[n][0] == P]


def program(nc, a, shapes, out, phases):
    T_ALL = a["x"].shape[1]
    NT = T_ALL // TILE
    ctx = ExitStack()
    with ctx:
        def sb(name, shape, dt=F32):
            return ctx.enter_context(nc.sbuf_tensor(name, shape, dt))

        banks = [ctx.enter_context(nc.psum_tensor(f"bank{i}", [P, TILE], F32)) for i in range(8)]
        x = sb("x_sb", [P, T_ALL])
        eps = sb("eps", [P, 1])
        kept, cut = {}, {}
        packs = {}
        for pack, names in (("first", first_names(shapes)), ("others", other_names(shapes))):
            packs[pack] = sb("k_" + pack, list(a[pack].shape))
            at = 0
            for name in names:
                size = math.prod(shapes[name][1:])
                view = packs[pack][:, at:at + size]
                kept[name] = view if len(shapes[name]) == 2 else view.rearrange("p (a b) -> p a b", b=shapes[name][2])
                at += size
        ones, ident = Ones(kept["c_ones"], eps), kept["c_ident"]
        ident16 = sb("ident16", [P, P], BF16)
        first_layer = ("m1_w1", "m1_w2", "m1_b2")
        late_layers = {"l2": ("m2_wg", "m2_wu", "m2_wd"), "l3": ("m3_wg", "m3_wu", "m3_wd")}
        sel8, sel16 = sb("sel8", [24, 8, P], BF16), sb("sel16", [48, 8, P], BF16)
        once = ("c_sel8", "c_sel16")
        alone = [n for n in a if n not in once + first_layer + late_layers["l2"] + late_layers["l3"] + ("x",) +
                 tuple(packs)]
        for name in alone:
            kept[name] = sb("k_" + name, list(a[name].shape), a[name].dtype)

        twice_bo = sb("twice_bo", [P, 1])
        wide0 = {n: sb(n, [P, 1]) for n in ("b_r", "b_z", "b_ssm")}
        wide = {"turns": sb("turns", [P, 4]), "factor": sb("factor", [P, 4]), "half_b2": sb("half_b2", [P, 1])}
        first_moe = ctx.enter_context(ExitStack())
        for name in first_layer:
            cut[name] = [first_moe.enter_context(nc.sbuf_tensor(f"{name}_{part}", list(shapes[name]), F32R))
                         for part in ("high", "low")]
        loaded = ctx.enter_context(nc.semaphore("loaded"))
        stored = ctx.enter_context(nc.semaphore("stored"))
        highs = ctx.enter_context(nc.semaphore("highs"))
        late_loaded = {ph: ctx.enter_context(nc.semaphore("late_loaded_" + ph)) for ph in ("l2", "l3")}
        loaded_first = ctx.enter_context(nc.semaphore("loaded_first"))
        start = ctx.enter_context(ExitStack())
        loads = {name: kept[name] for name in alone}
        for name in cut:
            loads[name] = start.enter_context(nc.sbuf_tensor("k_" + name, list(a[name].shape), F32))
        with ExitStack() as here:
            wide_sel = {name: here.enter_context(nc.sbuf_tensor("k_" + name, list(a[name].shape), F32)) for name in once}
            block = here.enter_context(nc.Block())

            @block.sync
            def _(sp):
                sp.dma_start(packs["first"][:, :], a["first"]).then_inc(loaded_first, 16)
                for name, tensor in wide_sel.items():
                    sp.dma_start(every(tensor), a[name]).then_inc(loaded_first, 16)
                sp.dma_start(x[:, :], a["x"]).then_inc(loaded_first, 16)
                sp.dma_start(packs["others"][:, :], a["others"]).then_inc(loaded, 16)
                for name, tensor in loads.items():
                    sp.dma_start(every(tensor), a[name]).then_inc(loaded, 16)

            @block.vector
            def _(dv):
                dv.memset(eps[:, :], EPS)
                dv.wait_ge(loaded_first, 16 * (2 + len(wide_sel)))
                dv.tensor_copy(ident16[:, :], ident[:, :])
                dv.tensor_copy(sel8[:, :, :], wide_sel["c_sel8"][:, :, :])
                dv.tensor_copy(sel16[:, :, :], wide_sel["c_sel16"][:, :, :])

        def prepare():
            with nc.Block() as block:
                @block.vector
                def _(dv):
                    dv.wait_ge(loaded, 16 * (1 + len(loads)))
                    for n, at in (("b_r", 0), ("b_z", 1)):
                        dv.tensor_tensor(wide0[n][:, :], kept["a0_b_ih"][:, at:at + 1], kept["a0_b_hh"][:, at:at + 1],
                                         ALU.add)
                    dv.tensor_tensor(wide0["b_ssm"][:, :], kept["a0_cb"][:, :], kept["a0_db"][:, :], ALU.add)
                    dv.tensor_scalar(twice_bo[:, :], kept["a2_bo"][:, :], 2.0, None, ALU.mult)
                    for n, name in enumerate(cut):
                        dv.wait_ge(highs, n + 1)
                        dv.tensor_tensor(every(cut[name][1]), every(loads[name]), every(cut[name][0]).bitcast(F32),
                                         ALU.subtract)

                @block.scalar
                def _(ac):
                    ac.wait_ge(loaded, 16 * (1 + len(loads)))
                    for name in cut:
                        ac.activation(every(cut[name][0]), every(loads[name]), ACT.Copy).then_inc(highs, 1)
            start.close()

        l1 = Moe(8, 8, [u // 4 for u in range(32)], False, False, kept["m1_gate"], cut["m1_w1"],
                 gate_b=kept["m1_gate_b"], down_w=cut["m1_w2"], bias=kept["m1_b1"], bias_down=cut["m1_b2"],
                 sel=sel8, rev=kept["c_rev8"], at=(3, 6, 16, 17, 27), margin_after=4,
                 at_update=1, lead=[4] * 8)
        ffn_w = {n: kept["f0_" + n] for n in ("theta", "wr", "wi", "b1", "w1", "w2", "b2")}
        quantum_constants(nc, ffn_w, wide, "qc")
        of_end, of_layer, cut_for, late = ctx.enter_context(ExitStack()), ctx.enter_context(ExitStack()), None, {}
        for i, ph in enumerate(phases):
            tag = f"p{i}"
            if i == (1 if phases[0] == "f0" else 0):
                prepare()
            if ph == "f0":
                with Signals(nc, tag, NORM_SIGNALS + FFN_SIGNALS) as sg:
                    ffn_pass(nc, x, ones, ident, banks, ffn_w, wide, sg, NT, tag)
            if ph == "a3":
                with Signals(nc, tag, NORM_SIGNALS + A3_SIGNALS) as sg, Signals(nc, tag + "n", NORM_SIGNALS) as sg2:
                    channel_gla_pass(nc, x, ones, ident, banks, {n[3:]: kept[n] for n in kept if n[:3] == "a3_"}, sg, sg2,
                                     NT, tag)
            if ph == "a1":
                with Signals(nc, tag, NORM_SIGNALS + A1_SIGNALS) as sg:
                    head_gla_pass(nc, x, ones, ident, banks, {n[3:]: kept[n] for n in kept if n[:3] == "a1_"}, sg, NT, tag)
            if ph == "a2":
                with Signals(nc, tag, WIDE_NORM_SIGNALS + A2_SIGNALS) as sg:
                    window_attention_pass(nc, x, ones, ident, banks, {n[3:]: kept[n] for n in kept if n[:3] == "a2_"},
                                          twice_bo, sg, NT, tag)
            if ph == "a0":
                with Signals(nc, tag, NORM_SIGNALS + A0_SIGNALS) as sg:
                    recurrent_pass(nc, x, ones, ident, banks, {n[3:]: kept[n] for n in kept if n[:3] == "a0_"}, wide0,
                                   sg, T_ALL // SEQ, tag)
            if ph in ("l1", "l2", "l3"):
                if ph != "l1" and cut_for != ph:
                    of_layer.close()
                    if "l1" not in phases[i + 1:]:
                        first_moe.close()
                    if not late:
                        for name in late_layers["l3"]:
                            late[name] = of_end.enter_context(nc.sbuf_tensor("k_" + name, list(a[name].shape), F32))
                    for name in late_layers[ph]:
                        cut[name] = [of_layer.enter_context(nc.sbuf_tensor(f"{name}_{part}", list(a[name].shape), F32R))
                                     for part in ("high", "low")]
                    with ExitStack() as now:
                        here = dict(late)
                        for name in late_layers[ph]:
                            if name not in here:
                                here[name] = now.enter_context(nc.sbuf_tensor("k_" + name, list(a[name].shape), F32))
                        loads = []
                        if not cut_for:
                            loads = [(here[n], a[n], late_loaded[ph]) for n in late_layers[ph]]
                            if ph == "l2":
                                loads += [(late[n], a[n], late_loaded["l3"]) for n in late_layers["l3"]]
                        split_weights(nc, [(here[n], *cut[n]) for n in late_layers[ph]], late_loaded[ph], loads,
                                      tag + "s")
                    cut_for = ph
                layer = l1
                if ph == "l2":
                    layer = Moe(16, 8, list(range(8)) + [None], True, True, kept["m2_gate"], cut["m2_wg"],
                                up_w=cut["m2_wu"], down_w=cut["m2_wd"], sel=sel16, rev=kept["c_rev16"],
                                at=(1, 3, 6, 0, 7), margin_after=3, at_update=0, lead=[2] + [3] * 7, buffers=6, deep=True)
                if ph == "l3":
                    layer = Moe(8, 8, [u // 2 for u in range(16)], True, False, kept["m3_gate"], cut["m3_wg"],
                                up_w=cut["m3_wu"], down_w=cut["m3_wd"], sel=sel8, rev=kept["c_rev8"],
                                at=(1, 5, 13, 0, 14), margin_after=6, lead=[2] + [4] * 7, deep=True)
                with Signals(nc, tag, NORM_SIGNALS + MOE_SIGNALS) as sg:
                    moe_pass(nc, x, ones, ident, ident16, banks, layer, sg, NT, tag)

        with nc.Block() as block:
            @block.sync
            def _(sp):
                sp.dma_start(out, x[:, :]).then_inc(stored, 16)
                sp.wait_ge(stored, 16)


PHASES = ["f0", "a0", "f0", "l1", "a1", "l1", "l2", "a2", "l2", "l3", "a3", "l3"]


def lay_out(i):
    f = {k: np.asarray(v) for k, v in i.items()}
    a = {"x": np.ascontiguousarray(f["L0_attn_x"].reshape(-1, D).T)}
    a.update(constants())
    for n, name in (("theta", "quantum_phases"), ("wr", "quantum_weights_real"), ("wi", "quantum_weights_imag"),
                    ("b1", "b1")):
        a["f0_" + n] = np.ascontiguousarray(f["L0_ffn_" + name].reshape(4, P).T)
    a["f0_w1"] = f["L0_ffn_W1"].reshape(D, 4, P)
    a["f0_w2"] = np.ascontiguousarray(f["L0_ffn_W2"].reshape(4, P, D).transpose(1, 0, 2))
    a["f0_b2"] = f["L0_ffn_b2"][:, None]
    for n in ("wq", "wk", "wv", "wg", "wo"):
        a["a3_" + n] = f["L3_attn_W" + n[1:]]
    for n in ("bq", "bk", "bg", "bo", "gamma", "beta"):
        a["a3_" + n] = f["L3_attn_" + n][:, None]
    a["a3_bv"] = np.ascontiguousarray(np.broadcast_to(f["L3_attn_bv"], (P, 4, P)))
    for n in ("wq", "wk", "wv", "wgk"):
        a["a1_" + n] = f["L1_attn_W" + n[1:]]
    a["a1_wg"] = f["L1_attn_Wg"].reshape(D, 2, P)
    a["a1_wo"] = np.ascontiguousarray(f["L1_attn_Wo"].reshape(2, P, D).transpose(1, 0, 2))
    a["a1_bgk"] = np.ascontiguousarray(np.broadcast_to(f["L1_attn_bgk"], (P, 4, 4)))
    a["a1_gnorm"] = np.ascontiguousarray(np.concatenate([f["L1_attn_gnorm_w"]] * 2)[:, None])
    w3, b3 = f["L2_attn_in_proj_w"].reshape(3, D, D), f["L2_attn_in_proj_b"].reshape(3, D)
    for n, name in enumerate("qkv"):
        a["a2_w" + name] = np.ascontiguousarray(w3[n].T)
    a["a2_bq"], a["a2_bk"] = b3[0][:, None], b3[1][:, None]
    a["a2_bv"] = np.ascontiguousarray(np.broadcast_to(b3[2], (P, 4, P)))
    a["a2_wo"] = np.ascontiguousarray(f["L2_attn_out_w"].T)
    a["a2_bo"] = f["L2_attn_out_b"][:, None]
    def padded(v, rows, cols):
        return np.pad(v, ((0, rows - v.shape[0]), (0, cols - v.shape[1])))

    a["a0_a"] = padded(f["L0_attn_A"].T, P, P)
    a["a0_bw"] = padded(f["L0_attn_Bw"].T, P, P)
    a["a0_cw"] = padded(f["L0_attn_Cw"].T, P, P)
    a["a0_bb"] = padded(f["L0_attn_Bb"][:, None], P, 1)
    for n, name in (("dw", "Dw"), ("proj", "proj_w")):
        a["a0_" + n] = np.ascontiguousarray(f["L0_attn_" + name].T)
    for n in ("ih", "hh"):
        a["a0_w_" + n] = np.ascontiguousarray(f["L0_attn_W_" + n].T.reshape(P, 3, P))
        a["a0_b_" + n] = np.ascontiguousarray(f["L0_attn_b_" + n].reshape(3, P).T)
    a["a0_b_in"], a["a0_b_hn"] = (np.ascontiguousarray(a["a0_b_" + n][:, 2:3]) for n in ("ih", "hh"))
    for n, name in (("cb", "Cb"), ("db", "Db"), ("proj_b", "proj_b")):
        a["a0_" + n] = f["L0_attn_" + name][:, None]
    a["a0_gate"] = np.ascontiguousarray(np.broadcast_to(f["L0_attn_gate_w"].T[:, :, None], (D, 2, P)))
    a["a0_gate_b"] = np.ascontiguousarray(np.broadcast_to(f["L0_attn_gate_b"], (P, 2)))
    a["m1_gate"] = f["L1_ffn_gate_w"]
    a["m1_gate_b"] = np.ascontiguousarray(np.broadcast_to(f["L1_ffn_gate_b"], (P, 4, 8)))
    a["m1_w1"] = np.ascontiguousarray(f["L1_ffn_W1"].reshape(8, D, 4, P).transpose(1, 0, 2, 3).reshape(D, 32, P))
    a["m1_b1"] = np.ascontiguousarray(f["L1_ffn_b1"].reshape(32, P).T)
    a["m1_w2"] = np.ascontiguousarray(f["L1_ffn_W2"].reshape(32, P, D).transpose(1, 0, 2))
    a["m1_b2"] = np.ascontiguousarray(np.concatenate([f["L1_ffn_b2"]] * 3, 0))
    a["m2_gate"] = np.ascontiguousarray(f["L2_ffn_gate_w"].T)
    for n, w, s in (("m2_wg", "L2_ffn_w_gate", "L2_ffn_ws_gate"), ("m2_wu", "L2_ffn_w_up", "L2_ffn_ws_up")):
        pairs = f[w].transpose(1, 0, 2).reshape(D, 8, P)
        a[n] = np.ascontiguousarray(np.concatenate([pairs, f[s][:, None, :]], 1))
    a["m2_wd"] = np.ascontiguousarray(np.concatenate([f["L2_ffn_w_down"].reshape(8, P, D), f["L2_ffn_ws_down"][None]],
                                                     0).transpose(1, 0, 2))
    a["m3_gate"] = f["L3_ffn_moe_router"]
    w13 = f["L3_ffn_moe_w13"]
    a["m3_wg"] = np.ascontiguousarray(w13[:, :, :256].reshape(8, D, 2, P).transpose(1, 0, 2, 3).reshape(D, 16, P))
    a["m3_wu"] = np.ascontiguousarray(w13[:, :, 256:].reshape(8, D, 2, P).transpose(1, 0, 2, 3).reshape(D, 16, P))
    a["m3_wd"] = np.ascontiguousarray(f["L3_ffn_moe_w2"].reshape(16, P, D).transpose(1, 0, 2))
    return a


def kernel(**inputs):
    import concourse.bacc as _bacc
    from concourse.bass_utils import run_bass_kernel_spmd as _run

    shape = inputs["L0_attn_x"].shape
    laid = lay_out(inputs)
    shapes = {k: v.shape for k, v in laid.items()}
    for pack, names in (("first", first_names(shapes)), ("others", other_names(shapes))):
        laid[pack] = np.concatenate([laid.pop(n).reshape(P, -1) for n in names], 1)
    arrays = {f"in_{k}_dram": v for k, v in laid.items()}
    nc = _bacc.Bacc("TRN2", target_bir_lowering=False, num_devices=1)
    aps = {k[3:-5]: nc.dram_tensor(k, v.shape, mybir.dt.from_np(v.dtype), kind="ExternalInput").ap()
           for k, v in arrays.items()}
    out = nc.dram_tensor("out_0_dram", aps["x"].shape, F32, kind="ExternalOutput").ap()
    program(nc, aps, shapes, out, PHASES)
    r = _run(nc, [arrays], core_ids=[0])
    return np.ascontiguousarray(r.results[0]["out_0_dram"].T).reshape(shape)
```
